# Optimizing a Trainium2 kernel written in Bass

```python
import numpy as np
import jax
import jax.numpy as jnp

def _softmax(x, axis=-1):
    return jax.nn.softmax(x, axis=axis)

def _gelu(x):
    return jax.nn.gelu(x, approximate=True)

def _silu(x):
    return jax.nn.silu(x)

def _sigmoid(x):
    return jax.nn.sigmoid(x)

def _layernorm(x, axis=-1, eps=1e-05):
    m = jnp.mean(x, axis=axis, keepdims=True)
    v = jnp.var(x, axis=axis, keepdims=True)
    return (x - m) / jnp.sqrt(v + eps)

def _scatter_add(tgt, idx, src, axis=0):
    return tgt.at[idx].add(src)

def _segment_sum(src, seg, n):
    return jax.ops.segment_sum(src, seg, n)
kernel_name = 'mk_xattn_ffn_d1_seqx_r8_41d876'

def setup_inputs(seed: int=0):
    np.random.seed(seed)
    _w = jnp.asarray

    def _rec_inputs():
        import jax
        import jax.numpy as jnp
        _rk = jax.random.key(seed)
        x = 4.136e-05 + 0.9999 * jax.random.normal(jax.random.fold_in(_rk, 1), (4, 256, 256), jnp.float32)
        _lenS = 256 - jax.random.randint(jax.random.fold_in(_rk, 7), (4,), 0, max(1, 256 // 4) + 1, jnp.int32)
        _lenS2 = 256 - jax.random.randint(jax.random.fold_in(_rk, 8), (4,), 0, max(1, 256 // 4) + 1, jnp.int32)
        _ctx_1024P = jax.random.normal(jax.random.fold_in(_rk, 11), (4, 16, 128), jnp.float32)
        _ctx_1024c = jax.random.dirichlet(jax.random.fold_in(_rk, 511), 0.3 * jnp.ones((16,), jnp.float32), (4, 256))
        _ctx_1024t = jnp.einsum('bsk,bkd->bsd', _ctx_1024c, _ctx_1024P)
        _ctx_1024t = _ctx_1024t * jax.lax.rsqrt(jnp.mean(jnp.square(_ctx_1024t)) + 1e-12) * 0.953939
        ctx_1024 = -0.000292821 + 1.00034 * (_ctx_1024t + 0.3 * jax.random.normal(jax.random.fold_in(_rk, 611), (4, 256, 128), jnp.float32))
        return (x, ctx_1024)
    x, ctx_1024 = _rec_inputs()

    def _L0_xattn_setup():
        import jax, jax.numpy as jnp
        import numpy as np
        import math
        B, L, DM = (2, 256, 128)
        DS, DC, EXP = (16, 4, 2)
        DI = EXP * DM
        DR = math.ceil(DM / 16)
        DT_MIN, DT_MAX, DT_FLOOR = (0.001, 0.1, 0.0001)

        def _ssm_forward(hidden_states, z, in_proj_w, conv_w, conv_b, x_proj_w, dt_proj_w, dt_proj_b, A_log, D):
            b = hidden_states.shape[0]
            x = jnp.einsum('ed,bld->bel', in_proj_w, hidden_states)
            xp = jnp.pad(x, ((0, 0), (0, 0), (DC - 1, 0)))
            xc = jax.lax.conv_general_dilated(xp, conv_w[:, None, :], window_strides=(1,), padding='VALID', dimension_numbers=('NCH', 'OIH', 'NCH'), feature_group_count=DI)
            u = jax.nn.silu(xc + conv_b[None, :, None])
            x_dbl = jnp.einsum('ke,bel->bkl', x_proj_w, u)
            dt_lo = x_dbl[:, :DR]
            Bm = x_dbl[:, DR:DR + DS]
            Cm = x_dbl[:, DR + DS:]
            delta = jax.nn.softplus(jnp.einsum('er,brl->bel', dt_proj_w, dt_lo) + dt_proj_b[None, :, None])
            A = -jnp.exp(A_log)

            def step(state, xs):
                d_t, B_t, C_t, u_t = xs
                dA = jnp.exp(d_t[..., None] * A)
                state = state * dA + (d_t * u_t)[..., None] * B_t[:, None, :]
                y_t = jnp.einsum('ben,bn->be', state, C_t)
                return (state, y_t)
            xs = (jnp.moveaxis(delta, -1, 0), jnp.moveaxis(Bm, -1, 0), jnp.moveaxis(Cm, -1, 0), jnp.moveaxis(u, -1, 0))
            state0 = jnp.zeros((b, DI, DS), delta.dtype)
            _, ys = jax.lax.scan(step, state0, xs)
            y = jnp.moveaxis(ys, 0, -1)
            y = y + D[None, :, None] * u
            y = y * jax.nn.silu(z)
            return jnp.swapaxes(y, 1, 2)
        key = jax.random.key(seed)
        ks = jax.random.split(key, 8)
        hidden_states = jax.random.normal(ks[0], (B, L, DM), jnp.float32)
        z = jax.random.normal(ks[1], (B, DI, L), jnp.float32)
        in_proj_w = jax.random.normal(ks[2], (DI, DM), jnp.float32) * DM ** (-0.5)
        conv_w = jax.random.normal(ks[3], (DI, DC), jnp.float32) * DC ** (-0.5)
        conv_b = jnp.zeros((DI,), jnp.float32)
        x_proj_w = jax.random.normal(ks[4], (DR + 2 * DS, DI), jnp.float32) * DI ** (-0.5)
        dt_std = DR ** (-0.5)
        dt_proj_w = jax.random.uniform(ks[5], (DI, DR), jnp.float32, -dt_std, dt_std)
        dt = jnp.exp(jax.random.uniform(ks[6], (DI,), jnp.float32) * (math.log(DT_MAX) - math.log(DT_MIN)) + math.log(DT_MIN))
        dt = jnp.clip(dt, DT_FLOOR)
        dt_proj_b = dt + jnp.log(-jnp.expm1(-dt))
        A_log = jnp.log(jnp.broadcast_to(jnp.arange(1, DS + 1, dtype=jnp.float32), (DI, DS)))
        D = jnp.ones((DI,), jnp.float32)
        return dict(hidden_states=hidden_states, z=z, in_proj_w=in_proj_w, conv_w=conv_w, conv_b=conv_b, x_proj_w=x_proj_w, dt_proj_w=dt_proj_w, dt_proj_b=dt_proj_b, A_log=A_log, D=D)
    _L0_xattn_all = _L0_xattn_setup()
    _L0_xattn_in = {k: v for k, v in _L0_xattn_all.items() if k in ('in_proj_w', 'conv_w', 'conv_b', 'x_proj_w', 'dt_proj_w', 'dt_proj_b', 'A_log', 'D')}
    del _L0_xattn_all

    def _L0_ffn_setup():
        import jax, jax.numpy as jnp
        import numpy as np
        E = 8
        TOPK = 2
        H = 256
        I = 512
        B, S = (2, 256)

        def _swiglu(x, gw, uw, dw):
            return jax.nn.silu(x @ gw) * (x @ uw) @ dw
        key = jax.random.key(seed)
        ks = jax.random.split(key, 8)
        s = 1.0 / np.sqrt(H)
        si = 1.0 / np.sqrt(I)
        return {'hidden_states': jax.random.normal(ks[0], (B, S, H), dtype=jnp.float32), 'wg': jax.random.normal(ks[1], (E, H), dtype=jnp.float32) * s, 'gate_w': jax.random.normal(ks[2], (E, H, I), dtype=jnp.float32) * s, 'up_w': jax.random.normal(ks[3], (E, H, I), dtype=jnp.float32) * s, 'down_w': jax.random.normal(ks[4], (E, I, H), dtype=jnp.float32) * si, 'shared_gate_w': jax.random.normal(ks[5], (H, I), dtype=jnp.float32) * s, 'shared_up_w': jax.random.normal(ks[6], (H, I), dtype=jnp.float32) * s, 'shared_down_w': jax.random.normal(ks[7], (I, H), dtype=jnp.float32) * si}
    _L0_ffn_all = _L0_ffn_setup()
    _L0_ffn_in = {k: v for k, v in _L0_ffn_all.items() if k in ('wg', 'gate_w', 'up_w', 'down_w', 'shared_gate_w', 'shared_up_w', 'shared_down_w')}
    del _L0_ffn_all
    return {'x': x, 'ctx_1024': ctx_1024, 'L0_xattn_in_proj_w': _L0_xattn_in['in_proj_w'], 'L0_xattn_conv_w': _L0_xattn_in['conv_w'], 'L0_xattn_conv_b': _L0_xattn_in['conv_b'], 'L0_xattn_x_proj_w': _L0_xattn_in['x_proj_w'], 'L0_xattn_dt_proj_w': _L0_xattn_in['dt_proj_w'], 'L0_xattn_dt_proj_b': _L0_xattn_in['dt_proj_b'], 'L0_xattn_A_log': _L0_xattn_in['A_log'], 'L0_xattn_D': _L0_xattn_in['D'], 'L0_ffn_wg': _L0_ffn_in['wg'], 'L0_ffn_gate_w': _L0_ffn_in['gate_w'], 'L0_ffn_up_w': _L0_ffn_in['up_w'], 'L0_ffn_down_w': _L0_ffn_in['down_w'], 'L0_ffn_shared_gate_w': _L0_ffn_in['shared_gate_w'], 'L0_ffn_shared_up_w': _L0_ffn_in['shared_up_w'], 'L0_ffn_shared_down_w': _L0_ffn_in['shared_down_w']}

def reference(x, ctx_1024, L0_xattn_in_proj_w, L0_xattn_conv_w, L0_xattn_conv_b, L0_xattn_x_proj_w, L0_xattn_dt_proj_w, L0_xattn_dt_proj_b, L0_xattn_A_log, L0_xattn_D, L0_ffn_wg, L0_ffn_gate_w, L0_ffn_up_w, L0_ffn_down_w, L0_ffn_shared_gate_w, L0_ffn_shared_up_w, L0_ffn_shared_down_w):
    import jax
    import jax.numpy as jnp

    def _L0_xattn_ref(hidden_states, z, in_proj_w, conv_w, conv_b, x_proj_w, dt_proj_w, dt_proj_b, A_log, D):
        import jax, jax.numpy as jnp
        import numpy as np
        import math
        B, L, DM = (2, 256, 128)
        DS, DC, EXP = (16, 4, 2)
        DI = EXP * DM
        DR = math.ceil(DM / 16)
        DT_MIN, DT_MAX, DT_FLOOR = (0.001, 0.1, 0.0001)

        def _ssm_forward(hidden_states, z, in_proj_w, conv_w, conv_b, x_proj_w, dt_proj_w, dt_proj_b, A_log, D):
            b = hidden_states.shape[0]
            x = jnp.einsum('ed,bld->bel', in_proj_w, hidden_states)
            xp = jnp.pad(x, ((0, 0), (0, 0), (DC - 1, 0)))
            xc = jax.lax.conv_general_dilated(xp, conv_w[:, None, :], window_strides=(1,), padding='VALID', dimension_numbers=('NCH', 'OIH', 'NCH'), feature_group_count=DI)
            u = jax.nn.silu(xc + conv_b[None, :, None])
            x_dbl = jnp.einsum('ke,bel->bkl', x_proj_w, u)
            dt_lo = x_dbl[:, :DR]
            Bm = x_dbl[:, DR:DR + DS]
            Cm = x_dbl[:, DR + DS:]
            delta = jax.nn.softplus(jnp.einsum('er,brl->bel', dt_proj_w, dt_lo) + dt_proj_b[None, :, None])
            A = -jnp.exp(A_log)

            def step(state, xs):
                d_t, B_t, C_t, u_t = xs
                dA = jnp.exp(d_t[..., None] * A)
                state = state * dA + (d_t * u_t)[..., None] * B_t[:, None, :]
                y_t = jnp.einsum('ben,bn->be', state, C_t)
                return (state, y_t)
            xs = (jnp.moveaxis(delta, -1, 0), jnp.moveaxis(Bm, -1, 0), jnp.moveaxis(Cm, -1, 0), jnp.moveaxis(u, -1, 0))
            state0 = jnp.zeros((b, DI, DS), delta.dtype)
            _, ys = jax.lax.scan(step, state0, xs)
            y = jnp.moveaxis(ys, 0, -1)
            y = y + D[None, :, None] * u
            y = y * jax.nn.silu(z)
            return jnp.swapaxes(y, 1, 2)
        return _ssm_forward(hidden_states, z, in_proj_w, conv_w, conv_b, x_proj_w, dt_proj_w, dt_proj_b, A_log, D)

    def _L0_ffn_ref(hidden_states, wg, gate_w, up_w, down_w, shared_gate_w, shared_up_w, shared_down_w):
        import jax, jax.numpy as jnp
        import numpy as np
        E = 8
        TOPK = 2
        H = 256
        I = 512
        B, S = (2, 256)

        def _swiglu(x, gw, uw, dw):
            return jax.nn.silu(x @ gw) * (x @ uw) @ dw
        b, s, h = hidden_states.shape
        x = hidden_states.reshape(-1, h)
        shared_out = _swiglu(x, shared_gate_w, shared_up_w, shared_down_w)
        logits = x.astype(jnp.float32) @ wg.T
        probs = jax.nn.softmax(logits, axis=-1)
        topw, sel = jax.lax.top_k(probs, TOPK)
        topw = topw / jnp.sum(topw, axis=-1, keepdims=True)
        topw = topw.astype(hidden_states.dtype)
        expert_w = jnp.sum(topw[..., None] * jax.nn.one_hot(sel, E, dtype=topw.dtype), axis=1)
        out = jnp.zeros_like(x)
        for e in range(E):
            y = _swiglu(x, gate_w[e], up_w[e], down_w[e])
            out = out + y * expert_w[:, e:e + 1]
        return (out + shared_out).reshape(b, s, h)
    x = x + _L0_xattn_ref(ctx_1024, _layernorm(x, axis=-1), L0_xattn_in_proj_w, L0_xattn_conv_w, L0_xattn_conv_b, L0_xattn_x_proj_w, L0_xattn_dt_proj_w, L0_xattn_dt_proj_b, L0_xattn_A_log, L0_xattn_D)
    x = x + _L0_ffn_ref(_layernorm(x, axis=-1), L0_ffn_wg, L0_ffn_gate_w, L0_ffn_up_w, L0_ffn_down_w, L0_ffn_shared_gate_w, L0_ffn_shared_up_w, L0_ffn_shared_down_w)
    return x

_drawn_inputs = setup_inputs


def setup_inputs(seed=0):
    import zlib

    import numpy as np

    out = dict(_drawn_inputs(seed))
    spreads = {'L0_xattn_conv_b': (0.0, 0.1), 'L0_xattn_D': (1.0, 0.2)}
    factors = {}
    for name, (base, spread) in spreads.items():
        noise = np.random.default_rng([zlib.crc32(name.encode()), seed]).standard_normal(out[name].shape)
        drawn = base * np.exp(spread * noise) if base else spread * noise
        out[name] = jnp.asarray(drawn.astype(out[name].dtype))
    for name, factor in factors.items():
        out[name] = (out[name] * factor).astype(out[name].dtype)
    return out
```

```python
from contextlib import ExitStack

import concourse.bass as bass
from concourse import mybir

F32 = mybir.dt.float32
I32 = mybir.dt.int32
ALU = mybir.AluOpType
ACT = mybir.ActivationFunctionType
AX_X = mybir.AxisListType.X

P = 128
B = 4
L = 256
TL = L // P
DM = 128
H = 256
KH = H // P
NS = 16
DR = 8
DC = 4
I = 512
E = 8
EPS = 1e-5
HALF = 2
IC = I // P // HALF
SLOTS = (E + 1) * HALF
PAIRS = NS // 2
UNITS = PAIRS * KH
W_GATE, W_UP, W_DOWN = 0, KH * I, 2 * KH * I
W_COLS = 2 * KH * I + (I // P) * H
SEED = 0x5F3759DF

C_IDENT = 0
C_RANK = C_IDENT + P
C_CONVW = C_RANK + E
C_CONVB = C_CONVW + KH * DC
C_DTB = C_CONVB + KH
C_ALOG = C_DTB + KH
C_D = C_ALOG + KH * NS
C_INW = C_D + KH
C_XPW = C_INW + H
C_WG = C_XPW + KH * (DR + 2 * NS)
C_END = C_WG + KH * E

ORDER = [E] + list(range(E))
PLAN = {s: [] for s in range(SLOTS)}
FIRST_UNIT_SLOT, LAST_UNIT_SLOT = 3, 14


def plan_units():
    slots = list(range(FIRST_UNIT_SLOT, LAST_UNIT_SLOT + 1))
    twice = UNITS - len(slots)
    v = 0
    for n, s in enumerate(slots):
        for _ in range(2 if n % 3 == 0 and n // 3 < twice else 1):
            PLAN[s].append(v)
            v += 1
    assert v == UNITS and all(v % KH == 0 for units in PLAN.values() for v in units[:1] if len(units) > 1)


plan_units()


def build(nc, x, ctx_t, params, dt_w, weights, out):
    with ExitStack() as stack:
        def sb(name, shape, dt=F32):
            return stack.enter_context(nc.sbuf_tensor(name, shape, dt))

        def ps(name, shape):
            return stack.enter_context(nc.psum_tensor(name, shape, F32))

        def sem(name):
            return stack.enter_context(nc.semaphore(name))

        w_sb = sb("w_sb", [P, E + 1, W_COLS])
        par = sb("par", [P, C_END])
        dtw = sb("dtw", [DR, H])
        x_sb = sb("x_sb", [P, B, TL, H])
        ctx_sb = sb("ctx_sb", [P, B, L])
        x2_t = sb("x2_t", [P, B, KH, L])
        convw = sb("convw", [P, KH, DC])
        convb = sb("convb", [P, KH])
        a_neg = sb("a_neg", [P, KH, NS])
        x_pad = sb("x_pad", [P, KH, DC - 1 + L])
        conv = sb("conv", [P, KH, L])
        tanh_u = sb("tanh_u", [P, KH, L])
        u = sb("u", [P, KH, L])
        bc_rows = sb("bc_rows", [2 * NS, L])
        dt_rows = sb("dt_rows", [DR, L])
        step_v = sb("step_v", [P, KH, L])
        step_abs = sb("step_abs", [P, KH, L])
        step_e = sb("step_e", [P, KH, L])
        step_w = sb("step_w", [P, KH, L])
        step_ln = sb("step_ln", [P, KH, L])
        delta = sb("delta", [P, KH, L])
        du = sb("du", [P, KH, L])
        z = sb("z", [P, KH, H])
        tanh_z = sb("tanh_z", [P, KH, H])
        gate2 = sb("gate2", [P, KH, H])
        decay = [sb(f"decay{i}", [P, 2, L]) for i in range(2)]
        drive = [sb(f"drive{i}", [P, 2, L]) for i in range(2)]
        state = [sb(f"state{i}", [P, 2, L]) for i in range(2)]
        part = [sb(f"part{i}", [P, 2, L]) for i in range(2)]
        wait_col = sb("wait_col", [P, 1])
        zero_col = sb("zero_col", [P, KH])
        y_acc = sb("y_acc", [P, KH, 2, L])
        yg = sb("yg", [P, KH, L])
        x2 = sb("x2", [P, TL, H])
        x2_s = sb("x2_s", [P, KH, L])
        stats = sb("stats", [P, 2, 6])
        mv = sb("mv", [P, 2, 2])
        ve = sb("ve", [P, 2])
        yi = sb("yi", [P, 2], I32)
        nr = sb("nr", [P, 2])
        logit = sb("logit", [P, TL, E])
        prob = sb("prob", [P, TL, E])
        pick = sb("pick", [P, TL, E])
        pick2 = sb("pick2", [P, TL, E])
        rest = sb("rest", [P, TL, E])
        small = sb("small", [P, 6, TL])
        wts = sb("wts", [P, TL, E])
        tanh_g = [sb(f"tanh_g{i}", [P, IC, L]) for i in range(2)]
        gated = [sb(f"gated{i}", [P, IC, L]) for i in range(2)]
        hid = [sb(f"hid{i}", [P, IC, L]) for i in range(2)]

        ident = par[:, C_IDENT:C_IDENT + P]
        rank = par[:, C_RANK:C_RANK + E]
        dt_b = par[:, C_DTB:C_DTB + KH]
        a_log = par[:, C_ALOG:C_ALOG + KH * NS]
        d_skip = par[:, C_D:C_D + KH]
        in_w = par[:, C_INW:C_INW + H]
        xp_w = par[:, C_XPW:C_XPW + KH * (DR + 2 * NS)].rearrange("p (k c) -> p k c", k=KH)
        wg = par[:, C_WG:C_WG + KH * E].rearrange("p (k e) -> p k e", k=KH)

        ps_gate = [ps(f"ps_gate{i}", [P, IC, L]) for i in range(2)]
        ps_up = [ps(f"ps_up{i}", [P, IC, L]) for i in range(2)]
        ps_y = ps("ps_y", [P, TL, H])
        ps_b = ps("ps_b", [P, 2, L])
        ps_c = ps("ps_c", [P, 2, L])
        ps_m = ps("ps_m", [P, 2, L])

        par_in = sem("par_in")
        x0_in = sem("x0_in")
        rest_in = sem("rest_in")
        w_in = [sem(f"w_in{e}") for e in range(E + 1)]
        setup_pool = sem("setup_pool")
        setup_exp = sem("setup_exp")
        setup_dve = sem("setup_dve")
        xin_done = sem("xin_done")
        xpad_done = sem("xpad_done")
        conv_done = sem("conv_done")
        tanh_u_done = sem("tanh_u_done")
        u_done = sem("u_done")
        xdbl_done = sem("xdbl_done")
        rows_done = sem("rows_done")
        dtp_done = sem("dtp_done")
        abs_done = sem("abs_done")
        step_exp_done = sem("step_exp_done")
        step_w_done = sem("step_w_done")
        ln_done = sem("ln_done")
        delta_done = sem("delta_done")
        du_done = sem("du_done")
        z_done = sem("z_done")
        tanh_z_done = sem("tanh_z_done")
        acc_ready = sem("acc_ready")
        yg_done = sem("yg_done")
        yt_done = sem("yt_done")
        x2_done = sem("x2_done")
        x2t_done = sem("x2t_done")
        x2_kept = sem("x2_kept")
        x2_fixed = sem("x2_fixed")
        logits_done = sem("logits_done")
        shifted = sem("shifted")
        exp_done = sem("exp_done")
        out_stored = sem("out_stored")
        pre_link = sem("pre_link")
        post_link = sem("post_link")
        bc_done = sem("bc_done")
        decay_done = sem("decay_done")
        drive_done = sem("drive_done")
        scan_done = sem("scan_done")
        part_done = sem("part_done")
        sum_done = sem("sum_done")
        gu_done = sem("gu_done")
        tanh_done = sem("tanh_done")
        gated_done = sem("gated_done")
        hid_done = sem("hid_done")
        down_done = sem("down_done")
        y_taken = sem("y_taken")

        PRE_LINKS = 2 + 12 + (DC - 1) + 2
        POST_LINKS = 2 + 2 + 12 + 21

        block = stack.enter_context(nc.Block())

        @block.sync
        def _(sp):
            sp.dma_start(par[:, :], params).then_inc(par_in, 16)
            sp.dma_start(dtw[:, :], dt_w).then_inc(par_in, 16)
            sp.dma_start(ctx_sb[:, 0, :], ctx_t[:, 0, :]).then_inc(x0_in, 16)
            x_tiles = x.rearrange("b (t p) h -> p b t h", p=P)
            out_tiles = out.rearrange("b (t p) h -> p b t h", p=P)
            sp.dma_start(x_sb[:, 0], x_tiles[:, 0]).then_inc(x0_in, 16)
            sp.dma_start(ctx_sb[:, 1:B, :], ctx_t[:, 1:B, :]).then_inc(rest_in, 16)
            for b in range(1, B):
                sp.dma_start(x_sb[:, b], x_tiles[:, b]).then_inc(rest_in, 16)
            for e in ORDER:
                sp.dma_start(w_sb[:, e, :], weights[e]).then_inc(w_in[e], 16)
            with sp.Fori(0, B) as b:
                sp.wait_ge(y_taken, b * (E + 1) + E + 2)
                sp.dma_start(out_tiles[:, b], x_sb[:, b]).then_inc(out_stored, 16)
            sp.wait_ge(out_stored, 16 * B)

        @block.tensor
        def _(pe):
            def in_proj(b):
                if not (isinstance(b, int) and b == 0):
                    pe.wait_ge(part_done, b * UNITS)
                for k in range(KH):
                    mm = nc.tensor.matmul(ps_c[:, k, :], in_w[:, k * P:(k + 1) * P], ctx_sb[:, b, :],
                                          start=(k == 0), stop=True, skip_group_check=True)
                mm.then_inc(xin_done, 1)

            def x_proj(b):
                pe.wait_ge(u_done, b + 1)
                for k in range(KH):
                    nc.tensor.matmul(ps_b[0:2 * NS, 0, :], xp_w[:, k, DR:DR + 2 * NS], u[:, k, :],
                                     start=(k == 0), stop=(k == KH - 1))
                for k in range(KH):
                    mm = nc.tensor.matmul(ps_b[0:DR, 1, :], xp_w[:, k, 0:DR], u[:, k, :],
                                          start=(k == 0), stop=(k == KH - 1))
                mm.then_inc(xdbl_done, 1)

            def dt_proj(b):
                pe.wait_ge(rows_done, b * 2 + 1)
                for k in range(KH):
                    mm = nc.tensor.matmul(ps_c[:, k, :], dtw[:, k * P:(k + 1) * P], dt_rows[:, :],
                                          start=(k == 0), stop=True, skip_group_check=True)
                mm.then_inc(dtp_done, 1)

            def spread(b, pair):
                if pair == 0:
                    pe.wait_ge(rows_done, b * 2 + 2)
                    pe.wait_ge(delta_done, b + 1)
                else:
                    pe.wait_ge(part_done, b * UNITS + pair * KH)
                for bank, first in ((ps_b, 0), (ps_c, NS)):
                    for i in range(2):
                        n = first + 2 * pair + i
                        mm = nc.tensor.matmul(bank[:, i, :],
                                              par[0:2 * NS, C_IDENT + n:C_IDENT + n + 1].to_broadcast([2 * NS, P]),
                                              bc_rows[:, :], start=(i == 0), stop=True, skip_group_check=True)
                mm.then_inc(bc_done, 1)

            def transpose_y(b):
                pe.wait_ge(yg_done, b + 1)
                for k in range(KH):
                    for t in range(TL):
                        mm = nc.tensor.transpose(ps_m[:, t, k * P:(k + 1) * P], yg[:, k, t * P:(t + 1) * P], ident)
                mm.then_inc(yt_done, 1)

            def transpose_x2(b):
                pe.wait_ge(x2_done, b + 1)
                for k in range(KH):
                    for t in range(TL):
                        mm = nc.tensor.transpose(ps_m[:, k, t * P:(t + 1) * P], x2[:, t, k * P:(k + 1) * P], ident)
                mm.then_inc(x2t_done, 1)

            def logits(b):
                pe.wait_ge(x2_kept, b + 1)
                pe.wait_ge(x2_fixed, b + 1)
                for t in range(TL):
                    for k in range(KH):
                        mm = nc.tensor.matmul(ps_m[:, 0, t * E:(t + 1) * E], x2_s[:, k, t * P:(t + 1) * P],
                                              wg[:, k, :], start=(t == 0 and k == 0), stop=(k == KH - 1),
                                              skip_group_check=True)
                mm.then_inc(logits_done, 1)

            def gate_up(fb, s):
                e, bank = ORDER[s // HALF], s % 2
                if s == 0:
                    pe.wait_ge(x2_kept, fb + 1)
                if s % HALF == 0:
                    pe.wait_ge(w_in[e], 16)
                pe.wait_ge(hid_done, fb * SLOTS + s + 1)
                for bank_ps, col in ((ps_gate[bank], W_GATE), (ps_up[bank], W_UP)):
                    for c in range(IC):
                        i0 = ((s % HALF) * IC + c) * P
                        for k in range(KH):
                            at = col + k * I + i0
                            mm = nc.tensor.matmul(bank_ps[:, c, :], w_sb[:, e, at:at + P], x2_t[:, fb, k, :],
                                                  start=(c == 0 and k == 0), stop=(k == KH - 1),
                                                  skip_group_check=True)
                mm.then_inc(gu_done, 1)

            def down(fb, s):
                e, bank = ORDER[s // HALF], s % 2
                if s % HALF == 0:
                    pe.wait_ge(y_taken, fb * (E + 1) + s // HALF + 1)
                pe.wait_ge(hid_done, fb * SLOTS + s + 3)
                for c in range(IC):
                    at = W_DOWN + ((s % HALF) * IC + c) * H
                    for t in range(TL):
                        mm = nc.tensor.matmul(ps_y[:, t, :], hid[bank][:, c, t * P:(t + 1) * P],
                                              w_sb[:, e, at:at + H],
                                              start=(s % HALF == 0 and c == 0 and t == 0),
                                              stop=(s % HALF == HALF - 1 and c == IC - 1), skip_group_check=True)
                mm.then_inc(down_done, 1)

            def batch(b, fb):
                for s in range(SLOTS):
                    if b is not None and s == 0:
                        in_proj(b)
                    if fb is not None:
                        gate_up(fb, s)
                    if b is not None:
                        for v in PLAN[s]:
                            if v % KH == 0:
                                spread(b, v // KH)
                    if b is not None and s == 1:
                        x_proj(b)
                    if fb is not None and s > 0:
                        down(fb, s - 1)
                    if b is not None and s == 1:
                        dt_proj(b)
                    if b is not None and s == LAST_UNIT_SLOT + 1:
                        transpose_y(b)
                    if b is not None and s == LAST_UNIT_SLOT + 2:
                        transpose_x2(b)
                if fb is not None:
                    down(fb, SLOTS - 1)
                if b is not None:
                    logits(b)

            pe.wait_ge(par_in, 32)
            pe.wait_ge(x0_in, 32)
            batch(0, None)
            pe.wait_ge(rest_in, 16 * B)
            with pe.Fori(1, B) as b:
                batch(b, b - 1)
            batch(None, B - 1)

        @block.scalar
        def _(act):
            def pre_pad(b):
                act.wait_ge(xin_done, b + 1)
                nc.scalar.copy(x_pad[:, :, DC - 1:], ps_c[:, :, :]).then_inc(xpad_done, 1)

            def pre_tanh(b):
                act.wait_ge(conv_done, b + 1)
                nc.scalar.activation(tanh_u[:, :, :], conv[:, :, :], ACT.Tanh).then_inc(tanh_u_done, 1)
                act.wait_ge(z_done, b + 1)
                nc.scalar.activation(tanh_z[:, :, :], z[:, :, :], ACT.Tanh, scale=0.5).then_inc(tanh_z_done, 1)

            def pre_rows(b):
                act.wait_ge(xdbl_done, b + 1)
                nc.scalar.copy(dt_rows[:, :], ps_b[0:DR, 1, :]).then_inc(rows_done, 1)
                nc.scalar.copy(bc_rows[:, :], ps_b[0:2 * NS, 0, :]).then_inc(rows_done, 1)

            def pre_delta(b):
                act.wait_ge(dtp_done, b + 1)
                for k in range(KH):
                    nc.scalar.activation(step_v[:, k, :], ps_c[:, k, :], ACT.Identity, bias=dt_b[:, k:k + 1])
                    ins = nc.scalar.activation(step_abs[:, k, :], ps_c[:, k, :], ACT.Abs, bias=dt_b[:, k:k + 1])
                ins.then_inc(abs_done, 1)
                act.wait_ge(abs_done, b + 1)
                nc.scalar.activation(step_e[:, :, :], step_abs[:, :, :], ACT.Exp, scale=-1.0).then_inc(step_exp_done, 1)
                act.wait_ge(step_w_done, b + 1)
                nc.scalar.activation(step_ln[:, :, :], step_w[:, :, :], ACT.Ln).then_inc(ln_done, 1)

            def unit_decay(b, v):
                k, pair = v % KH, v // KH
                if v == 0:
                    act.wait_ge(delta_done, b + 1)
                if not (isinstance(b, int) and b == 0 and v < 2):
                    act.wait_ge(scan_done, b * UNITS + v - 1)
                for i in range(2):
                    n = 2 * pair + i
                    ins = nc.scalar.activation(decay[v % 2][:, i, 1:L], delta[:, k, 1:L], ACT.Exp,
                                               scale=a_neg[:, k, n:n + 1])
                ins.then_inc(decay_done, 1)

            def keep_x2(b):
                act.wait_ge(x2t_done, b + 1)
                nc.scalar.copy(x2_t[:, b, :, :], ps_m[:, :, :]).then_inc(x2_kept, 1)

            def router_exp(b):
                act.wait_ge(shifted, b + 1)
                nc.scalar.activation(prob[:, :, :], logit[:, :, :], ACT.Exp).then_inc(exp_done, 1)

            def gate_tanh(fb, s):
                act.wait_ge(gu_done, fb * SLOTS + s + 1)
                nc.scalar.activation(tanh_g[s % 2][:, :, :], ps_gate[s % 2][:, :, :], ACT.Tanh,
                                     scale=0.5).then_inc(tanh_done, 1)

            def batch(b, fb):
                for s in range(SLOTS):
                    if b is not None:
                        for v in PLAN[s]:
                            unit_decay(b, v)
                        if s == 0:
                            pre_pad(b)
                    if fb is not None:
                        gate_tanh(fb, s)
                    if b is not None:
                        if s == 0:
                            pre_tanh(b)
                        if s == 1:
                            pre_rows(b)
                            pre_delta(b)
                        if s == LAST_UNIT_SLOT + 2:
                            keep_x2(b)
                if b is not None:
                    router_exp(b)

            act.wait_ge(par_in, 32)
            nc.scalar.activation(a_neg[:, :, :], a_log.rearrange("p (k n) -> p k n", k=KH), ACT.Exp).then_inc(setup_exp, 1)
            act.wait_ge(setup_dve, 3)
            act.wait_ge(setup_pool, 4)
            batch(0, None)
            with act.Fori(1, B) as b:
                batch(b, b - 1)
            batch(None, B - 1)

        @block.gpsimd
        def _(pool):
            nc.gpsimd.memset(x_pad[:, :, 0:DC - 1], 0.0).then_inc(setup_pool, 1)
            for i in range(2):
                nc.gpsimd.memset(decay[i][:, :, 0:1], 0.0).then_inc(setup_pool, 1)
            nc.gpsimd.memset(zero_col[:, :], 0.0).then_inc(setup_pool, 1)
            pool.wait_ge(par_in, 32)
            pool.wait_ge(setup_pool, 4)

            def start_sum(b):
                if not (isinstance(b, int) and b == 0):
                    pool.wait_ge(yg_done, b)
                zeros = zero_col[:, :].unsqueeze(2).to_broadcast([P, KH, L])
                nc.gpsimd.tensor_tensor(y_acc[:, :, 1, :], zeros, zeros, ALU.add)
                pool.wait_ge(u_done, b + 1)
                nc.gpsimd.tensor_tensor(y_acc[:, :, 0, :], u[:, :, :], d_skip.unsqueeze(2).to_broadcast([P, KH, L]),
                                        ALU.mult).then_inc(acc_ready, 1)
                pool.wait_ge(acc_ready, b + 1)

            def add_unit(b, v):
                pool.wait_ge(part_done, b * UNITS + v + 1)
                if not (isinstance(b, int) and b == 0 and v < 2):
                    pool.wait_ge(sum_done, b * UNITS + v - 1)
                nc.gpsimd.tensor_tensor(y_acc[:, v % KH], y_acc[:, v % KH], part[v % 2][:, :, :],
                                        ALU.add).then_inc(sum_done, 1)

            def batch(b):
                start_sum(b)
                for v in range(UNITS):
                    add_unit(b, v)

            batch(0)
            with pool.Fori(1, B) as b:
                batch(b)

        @block.vector
        def _(dve):
            links = {}

            def link(ins, chain, b, per):
                links[chain.name] = links.get(chain.name, 0) + 1
                ins.then_inc(chain, 1)
                dve.wait_ge(chain, b * per + links[chain.name])

            def rsqrt(b, chain, per):
                y = yi[:, :].bitcast(F32)
                link(nc.vector.tensor_scalar(ve[:, :], mv[:, :, 1], EPS, None, ALU.add), chain, b, per)
                link(nc.vector.tensor_scalar(yi[:, :], ve[:, :].bitcast(I32), 1, None, ALU.logical_shift_right),
                     chain, b, per)
                link(nc.vector.tensor_scalar(yi[:, :], yi[:, :], -1.0, float(SEED), ALU.mult, ALU.add), chain, b, per)
                for _ in range(3):
                    link(nc.vector.scalar_tensor_tensor(out=nr[:, :], in0=y, scalar=-0.5, in1=y, op0=ALU.mult,
                                                        op1=ALU.mult), chain, b, per)
                    link(nc.vector.tensor_tensor(nr[:, :], nr[:, :], ve[:, :], ALU.mult), chain, b, per)
                    link(nc.vector.scalar_tensor_tensor(out=y, in0=nr[:, :], scalar=1.5, in1=y, op0=ALU.add,
                                                        op1=ALU.mult), chain, b, per)
                return y

            def row_stats(b, chain, per):
                nc.vector.memset(wait_col[:, :], 0.0)
                for t in range(TL):
                    ins = nc.vector.bn_stats(stats[:, t, :], x_sb[:, b, t, :])
                link(ins, chain, b, per)
                nc.vector.memset(wait_col[:, :], 0.0)
                for t in range(TL):
                    ins = nc.vector.bn_aggr(mv[:, t, :], stats[:, t, :])
                link(ins, chain, b, per)

            def pre_norm(b):
                row_stats(b, pre_link, PRE_LINKS)
                y = rsqrt(b, pre_link, PRE_LINKS)
                for t in range(TL):
                    ins = nc.vector.tensor_scalar(z[:, t, :], x_sb[:, b, t, :], mv[:, t, 0:1], y[:, t:t + 1],
                                                  ALU.subtract, ALU.mult)
                ins.then_inc(z_done, 1)

            def pre_conv(b):
                dve.wait_ge(xpad_done, b + 1)
                for k in range(KH):
                    ins = nc.vector.tensor_scalar(conv[:, k, :], x_pad[:, k, 0:L], convw[:, k, 0:1],
                                                  convb[:, k:k + 1], ALU.mult, ALU.add)
                link(ins, pre_link, b, PRE_LINKS)
                for j in range(1, DC):
                    for k in range(KH):
                        ins = nc.vector.scalar_tensor_tensor(out=conv[:, k, :], in0=x_pad[:, k, j:j + L],
                                                             scalar=convw[:, k, j:j + 1], in1=conv[:, k, :],
                                                             op0=ALU.mult, op1=ALU.add)
                    if j < DC - 1:
                        link(ins, pre_link, b, PRE_LINKS)
                ins.then_inc(conv_done, 1)

            def pre_u(b):
                dve.wait_ge(tanh_u_done, b + 1)
                nc.vector.scalar_tensor_tensor(out=u[:, :, :], in0=tanh_u[:, :, :], scalar=1.0, in1=conv[:, :, :],
                                               op0=ALU.add, op1=ALU.mult).then_inc(u_done, 1)

            def pre_du(b):
                dve.wait_ge(tanh_z_done, b + 1)
                nc.vector.scalar_tensor_tensor(out=gate2[:, :, :], in0=tanh_z[:, :, :], scalar=1.0, in1=z[:, :, :],
                                               op0=ALU.add, op1=ALU.mult)
                dve.wait_ge(step_exp_done, b + 1)
                link(nc.vector.tensor_scalar(step_w[:, :, :], step_e[:, :, :], 1.0, None, ALU.add),
                     step_w_done, b, 1)
                link(nc.vector.scalar_tensor_tensor(out=step_e[:, :, :], in0=step_w[:, :, :], scalar=-1.0,
                                                    in1=step_e[:, :, :], op0=ALU.add, op1=ALU.subtract),
                     pre_link, b, PRE_LINKS)
                dve.wait_ge(ln_done, b + 1)
                link(nc.vector.tensor_tensor(step_e[:, :, :], step_ln[:, :, :], step_e[:, :, :], ALU.subtract),
                     pre_link, b, PRE_LINKS)
                nc.vector.scalar_tensor_tensor(out=delta[:, :, :], in0=step_v[:, :, :], scalar=0.0,
                                               in1=step_e[:, :, :], op0=ALU.max, op1=ALU.add).then_inc(delta_done, 1)
                dve.wait_ge(delta_done, b + 1)
                dve.wait_ge(u_done, b + 1)
                nc.vector.tensor_tensor(du[:, :, :], delta[:, :, :], u[:, :, :], ALU.mult).then_inc(du_done, 1)

            def unit_drive(b, v):
                if v == 0:
                    dve.wait_ge(du_done, b + 1)
                dve.wait_ge(bc_done, b * PAIRS + v // KH + 1)
                nc.vector.tensor_tensor(drive[v % 2][:, :, :], du[:, v % KH:v % KH + 1, :].to_broadcast([P, 2, L]),
                                        ps_b[:, :, :], ALU.mult).then_inc(drive_done, 1)

            def unit_scan(b, v):
                dve.wait_ge(drive_done, b * UNITS + v + 1)
                dve.wait_ge(decay_done, b * UNITS + v + 1)
                nc.vector.tensor_tensor_scan(state[v % 2][:, :, :].rearrange("p i l -> p (i l)"),
                                             decay[v % 2][:, :, :].rearrange("p i l -> p (i l)"),
                                             drive[v % 2][:, :, :].rearrange("p i l -> p (i l)"),
                                             0.0, ALU.mult, ALU.add).then_inc(scan_done, 1)

            def unit_part(b, v):
                dve.wait_ge(scan_done, b * UNITS + v + 1)
                if not (isinstance(b, int) and b == 0 and v < 2):
                    dve.wait_ge(sum_done, b * UNITS + v - 1)
                nc.vector.tensor_tensor(part[v % 2][:, :, :], state[v % 2][:, :, :], ps_c[:, :, :],
                                        ALU.mult).then_inc(part_done, 1)

            def post_gate(b):
                dve.wait_ge(sum_done, b * UNITS + UNITS)
                link(nc.vector.tensor_tensor(yg[:, :, :], y_acc[:, :, 0, :], y_acc[:, :, 1, :], ALU.add),
                     post_link, b, POST_LINKS)
                nc.vector.scalar_tensor_tensor(out=yg[:, :, :], in0=yg[:, :, :], scalar=0.5, in1=gate2[:, :, :],
                                               op0=ALU.mult, op1=ALU.mult).then_inc(yg_done, 1)

            def post_norm(b):
                dve.wait_ge(yt_done, b + 1)
                link(nc.vector.tensor_tensor(x_sb[:, b], x_sb[:, b], ps_m[:, :, :], ALU.add), post_link, b, POST_LINKS)
                row_stats(b, post_link, POST_LINKS)
                y = rsqrt(b, post_link, POST_LINKS)
                for t in range(TL):
                    ins = nc.vector.tensor_scalar(x2[:, t, :], x_sb[:, b, t, :], mv[:, t, 0:1], y[:, t:t + 1],
                                                  ALU.subtract, ALU.mult)
                ins.then_inc(x2_done, 1)

            def fix_x2(b):
                dve.wait_ge(x2_kept, b + 1)
                nc.vector.tensor_copy(x2_s[:, :, :], ps_m[:, :, :]).then_inc(x2_fixed, 1)

            def route(b):
                def step(ins):
                    link(ins, post_link, b, POST_LINKS)

                def wide(ap):
                    return ap.unsqueeze(2).to_broadcast([P, TL, E])

                ranks = rank.unsqueeze(1).to_broadcast([P, TL, E])
                top, total, first, second, mark, share = (small[:, n, :] for n in range(6))
                dve.wait_ge(logits_done, b + 1)
                lg = ps_m[:, 0, 0:TL * E].rearrange("p (t e) -> p t e", t=TL)
                step(nc.vector.tensor_reduce(top, lg, AX_X, ALU.max))
                nc.vector.tensor_tensor(logit[:, :, :], lg, wide(top), ALU.subtract).then_inc(shifted, 1)
                dve.wait_ge(exp_done, b + 1)
                step(nc.vector.tensor_reduce(total, prob[:, :, :], AX_X, ALU.add))
                step(nc.vector.reciprocal(total, total))
                step(nc.vector.tensor_tensor(prob[:, :, :], prob[:, :, :], wide(total), ALU.mult))
                step(nc.vector.tensor_reduce(first, prob[:, :, :], AX_X, ALU.max))
                step(nc.vector.tensor_tensor(pick[:, :, :], prob[:, :, :], wide(first), ALU.is_equal))
                step(nc.vector.tensor_tensor(pick[:, :, :], pick[:, :, :], ranks, ALU.mult))
                step(nc.vector.tensor_reduce(mark, pick[:, :, :], AX_X, ALU.max))
                step(nc.vector.tensor_tensor(pick[:, :, :], ranks, wide(mark), ALU.is_equal))
                step(nc.vector.scalar_tensor_tensor(out=rest[:, :, :], in0=pick[:, :, :], scalar=-2.0,
                                                    in1=prob[:, :, :], op0=ALU.mult, op1=ALU.add))
                step(nc.vector.tensor_reduce(second, rest[:, :, :], AX_X, ALU.max))
                step(nc.vector.tensor_tensor(pick2[:, :, :], rest[:, :, :], wide(second), ALU.is_equal))
                step(nc.vector.tensor_tensor(pick2[:, :, :], pick2[:, :, :], ranks, ALU.mult))
                step(nc.vector.tensor_reduce(mark, pick2[:, :, :], AX_X, ALU.max))
                step(nc.vector.tensor_tensor(pick2[:, :, :], ranks, wide(mark), ALU.is_equal))
                step(nc.vector.tensor_tensor(share, first, second, ALU.add))
                step(nc.vector.tensor_scalar(share, share, 2.0, None, ALU.mult))
                step(nc.vector.reciprocal(share, share))
                step(nc.vector.tensor_tensor(pick[:, :, :], pick[:, :, :], pick2[:, :, :], ALU.add))
                step(nc.vector.tensor_tensor(pick[:, :, :], pick[:, :, :], prob[:, :, :], ALU.mult))
                step(nc.vector.tensor_tensor(wts[:, :, :], pick[:, :, :], wide(share), ALU.mult))

            def gate_mul(fb, s):
                dve.wait_ge(tanh_done, fb * SLOTS + s + 1)
                nc.vector.scalar_tensor_tensor(out=gated[s % 2][:, :, :], in0=tanh_g[s % 2][:, :, :], scalar=1.0,
                                               in1=ps_gate[s % 2][:, :, :], op0=ALU.add,
                                               op1=ALU.mult).then_inc(gated_done, 1)

            def up_mul(fb, s):
                dve.wait_ge(gated_done, fb * SLOTS + s + 1)
                nc.vector.tensor_tensor(hid[s % 2][:, :, :], gated[s % 2][:, :, :], ps_up[s % 2][:, :, :],
                                        ALU.mult).then_inc(hid_done, 1)

            def add_expert(fb, n):
                dve.wait_ge(down_done, fb * SLOTS + HALF * n + HALF)
                for t in range(TL):
                    e = ORDER[n]
                    weight = 0.5 if e == E else wts[:, t, e:e + 1]
                    ins = nc.vector.scalar_tensor_tensor(out=x_sb[:, fb, t, :], in0=ps_y[:, t, :], scalar=weight,
                                                         in1=x_sb[:, fb, t, :], op0=ALU.mult, op1=ALU.add)
                ins.then_inc(y_taken, 1)

            def batch(b, fb):
                links.clear()
                for s in range(SLOTS):
                    if b is not None and s == 0:
                        pre_norm(b)
                        pre_conv(b)
                        pre_u(b)
                    if b is not None and s == LAST_UNIT_SLOT + 2:
                        post_norm(b)
                    units = PLAN[s] if b is not None else []
                    if fb is not None:
                        gate_mul(fb, s)
                    if units:
                        unit_drive(b, units[0])
                    if fb is not None:
                        up_mul(fb, s)
                    if units:
                        unit_scan(b, units[0])
                    if fb is not None and s % HALF == 0 and s > 0:
                        add_expert(fb, s // HALF - 1)
                    if units:
                        unit_part(b, units[0])
                    for v in units[1:]:
                        unit_drive(b, v)
                        unit_scan(b, v)
                        unit_part(b, v)
                    if b is not None:
                        if s == 1:
                            pre_du(b)
                        if s == LAST_UNIT_SLOT + 1:
                            post_gate(b)
                        if s == LAST_UNIT_SLOT + 2:
                            fix_x2(b)
                if fb is not None:
                    add_expert(fb, E)
                if b is not None:
                    route(b)
                    assert links[pre_link.name] == PRE_LINKS, links
                    assert links[post_link.name] == POST_LINKS, links

            dve.wait_ge(par_in, 32)
            nc.vector.tensor_scalar(convw[:, :, :], par[:, C_CONVW:C_CONVW + KH * DC].rearrange("p (k c) -> p k c", k=KH),
                                    0.5, None, ALU.mult).then_inc(setup_dve, 1)
            nc.vector.tensor_scalar(convb[:, :], par[:, C_CONVB:C_CONVB + KH], 0.5, None, ALU.mult).then_inc(setup_dve, 1)
            dve.wait_ge(setup_exp, 1)
            nc.vector.tensor_scalar(a_neg[:, :, :], a_neg[:, :, :], -1.0, None, ALU.mult).then_inc(setup_dve, 1)
            dve.wait_ge(setup_dve, 3)
            dve.wait_ge(x0_in, 32)
            dve.sem_inc(hid_done, 2)
            dve.sem_inc(y_taken, 1)
            batch(0, None)
            dve.wait_ge(rest_in, 16 * B)
            with dve.Fori(1, B) as b:
                batch(b, b - 1)
            batch(None, B - 1)


def kernel(x, ctx_1024, L0_xattn_in_proj_w, L0_xattn_conv_w, L0_xattn_conv_b, L0_xattn_x_proj_w,
           L0_xattn_dt_proj_w, L0_xattn_dt_proj_b, L0_xattn_A_log, L0_xattn_D, L0_ffn_wg, L0_ffn_gate_w,
           L0_ffn_up_w, L0_ffn_down_w, L0_ffn_shared_gate_w, L0_ffn_shared_up_w, L0_ffn_shared_down_w):
    import numpy as np
    import concourse.bacc as bacc
    from concourse.bass_utils import run_bass_kernel_spmd

    def halves(a):
        a = np.asarray(a).reshape(-1, P, int(np.prod(np.shape(a)[1:], dtype=int)))
        return a.transpose(1, 0, 2).reshape(P, -1)

    params = np.concatenate([
        np.eye(P, dtype=np.float32),
        np.tile(np.arange(E, 0, -1, dtype=np.float32), (P, 1)),
        halves(L0_xattn_conv_w), halves(L0_xattn_conv_b), halves(L0_xattn_dt_proj_b), halves(L0_xattn_A_log),
        halves(L0_xattn_D), np.asarray(L0_xattn_in_proj_w).T, halves(np.asarray(L0_xattn_x_proj_w).T),
        halves(np.asarray(L0_ffn_wg).T)], axis=1)
    gate = np.concatenate([np.asarray(L0_ffn_gate_w), np.asarray(L0_ffn_shared_gate_w)[None]])
    up = np.concatenate([np.asarray(L0_ffn_up_w), np.asarray(L0_ffn_shared_up_w)[None]])
    down = np.concatenate([np.asarray(L0_ffn_down_w), np.asarray(L0_ffn_shared_down_w)[None]])
    weights = np.stack([np.concatenate([halves(gate[e]), halves(up[e]), halves(down[e])], axis=1)
                        for e in range(E + 1)])
    arrays = {
        "x": np.ascontiguousarray(x),
        "ctx_t": np.ascontiguousarray(np.asarray(ctx_1024).transpose(2, 0, 1)),
        "params": np.ascontiguousarray(params),
        "dt_w": np.ascontiguousarray(np.asarray(L0_xattn_dt_proj_w).T),
        "weights": np.ascontiguousarray(weights),
    }
    nc = bacc.Bacc("TRN2", target_bir_lowering=False, num_devices=1)
    args = [nc.dram_tensor(name, a.shape, mybir.dt.from_np(a.dtype), kind="ExternalInput").ap()
            for name, a in arrays.items()]
    args.append(nc.dram_tensor("out", (B, L, H), F32, kind="ExternalOutput").ap())
    build(nc, *args)
    result = run_bass_kernel_spmd(nc, [arrays], core_ids=[0])
    return result.results[0]["out"]
```

```python
from contextlib import ExitStack

import concourse.bass as bass
from concourse import mybir

F32 = mybir.dt.float32
F32R = mybir.dt.float32r
BF16 = mybir.dt.bfloat16
I32 = mybir.dt.int32
ALU = mybir.AluOpType
ACT = mybir.ActivationFunctionType
AX_X = mybir.AxisListType.X

P = 128
B = 4
L = 256
TL = L // P
G = 2
GB = B // G
T = GB * L
TT = T // P
DM = 128
H = 256
KH = H // P
NS = 16
DR = 8
DC = 4
I = 512
E = 8
EPS = 1e-5
IC = I // P
X = E + 1
SLOTS = X * IC
UNITS = NS * KH
PAIR = 2 * IC
MATS = 3
MAT_COLS = KH * I
GATE, UP, DOWN = range(MATS)
BC = 2 * NS
PARTS = 3
SEED = 0x5F3759DF
CUTS = (2, 6, 10)
assert UNITS == (E // 2) * PAIR and (I // P) * H == MAT_COLS

C_IDENT = 0
C_RANK = C_IDENT + P
C_SEL = C_RANK + E
C_CONVB = C_SEL + BC
C_DTB = C_CONVB + KH
C_ALOG = C_DTB + KH
C_D = C_ALOG + KH * NS
C_INW = C_D + KH
C_XPW = C_INW + H
C_WG = C_XPW + KH * (DR + PARTS * BC)
C_TAPS = C_WG + KH * E
C_END = C_TAPS + DC * H


def build(nc, x, ctx_t, params, dt_w, weights, out):
    with ExitStack() as stack:
        def sb(name, shape, dt=F32):
            return stack.enter_context(nc.sbuf_tensor(name, shape, dt))

        def ps(name, shape):
            return stack.enter_context(nc.psum_tensor(name, shape, F32))

        def sem(name):
            return stack.enter_context(nc.semaphore(name))

        w_raw = [sb(f"w_raw{m}", [P, MAT_COLS]) for m in range(MATS)]
        w_hi = [[sb(f"w_hi{i}{m}", [P, MAT_COLS], F32R) for m in range(MATS)] for i in range(2)]
        w_lo = [[sb(f"w_lo{i}{m}", [P, MAT_COLS], F32R) for m in range(MATS)] for i in range(2)]
        par = sb("par", [P, C_END])
        dtw = sb("dtw", [DR, H])
        x_sb = sb("x_sb", [P, B, TL, H])
        ctx_sb = sb("ctx_sb", [P, B, DC - 1 + L])
        sel = sb("sel", [PARTS * BC, BC], BF16)
        convb = sb("convb", [P, KH])
        a_neg = sb("a_neg", [P, KH, NS])
        bufs = [sb(f"buf{i}", [P, KH, T]) for i in range(4)]
        conv_h, tanh_u, z, tanh_z = bufs
        step_v, step_abs, step_e, step_w = bufs[0], bufs[1], sb("step_e", [P, KH, T]), bufs[1]
        step_ln = sb("step_ln", [P, KH, T])
        rows = [sb(f"rows{g}", [PARTS * BC, T], BF16) for g in range(G)]
        row_rest = sb("row_rest", [PARTS * BC, T])
        row_mid = sb("row_mid", [PARTS * BC, T], BF16)
        dt_rows = sb("dt_rows", [DR, T])
        u = [sb(f"u{g}", [P, KH, T]) for g in range(G)]
        delta = [sb(f"delta{g}", [P, KH, T]) for g in range(G)]
        du = [sb(f"du{g}", [P, KH, T]) for g in range(G)]
        gate2 = [sb(f"gate2{g}", [P, KH, T]) for g in range(G)]
        decay = [sb(f"decay{i}", [P, GB, L]) for i in range(2)]
        drive = [sb(f"drive{i}", [P, T]) for i in range(KH)]
        state = [sb(f"state{i}", [P, T]) for i in range(KH)]
        part = [sb(f"part{i}", [P, T]) for i in range(2)]
        y_acc = sb("y_acc", [P, KH, T])
        yg = sb("yg", [P, KH, T])
        x2 = yg[:, :, :].rearrange("p k t -> p (k t)").rearrange("p (t h) -> p t h", t=TT)
        x2_s = step_ln
        x2_hi = [sb(f"x2_hi{g}", [P, KH, T], F32R) for g in range(G)]
        x2_lo = [sb(f"x2_lo{g}", [P, KH, T], F32R) for g in range(G)]
        stats = sb("stats", [P, TT, 6])
        mv = sb("mv", [P, TT, 2])
        ve = sb("ve", [P, TT])
        yi = sb("yi", [P, TT], I32)
        nr = sb("nr", [P, TT])
        logit = sb("logit", [P, TT, E])
        prob = sb("prob", [P, TT, E])
        pick = sb("pick", [P, TT, E])
        pick2 = sb("pick2", [P, TT, E])
        rest = sb("rest", [P, TT, E])
        small = sb("small", [P, 6, TT])
        wts = sb("wts", [P, TT, E])
        tanh_g = [sb(f"tanh_g{i}", [P, T]) for i in range(2)]
        gated = sb("gated", [P, T])
        hid = [sb(f"hid{i}", [P, T]) for i in range(2)]
        hid_hi = [sb(f"hid_hi{i}", [P, T], F32R) for i in range(2)]
        hid_lo = [sb(f"hid_lo{i}", [P, T], F32R) for i in range(2)]
        in_wk = sb("in_wk", [P, DC, H])

        ident = par[:, C_IDENT:C_IDENT + P]
        rank = par[:, C_RANK:C_RANK + E]
        dt_b = par[:, C_DTB:C_DTB + KH]
        d_skip = par[:, C_D:C_D + KH]
        in_w = par[:, C_INW:C_INW + H]
        xp_w = par[:, C_XPW:C_WG].rearrange("p (k c) -> p k c", k=KH)
        wg = par[:, C_WG:C_TAPS].rearrange("p (k e) -> p k e", k=KH)
        taps = par[:, C_TAPS:C_END].rearrange("p (j e) -> p j e", j=DC)

        ps_gate = [ps(f"ps_gate{i}", [P, T]) for i in range(2)]
        ps_up = [ps(f"ps_up{i}", [P, T]) for i in range(2)]
        ps_y = [ps(f"ps_y{i}", [P, TT // 2, H]) for i in range(2)]
        ps_b = ps("ps_b", [P, T])
        ps_c = ps("ps_c", [P, T])
        ps_m = [ps_b, ps_c]

        par_in, x0_in, rest_in = sem("par_in"), sem("x0_in"), sem("rest_in")
        w_in = [sem(f"w_in{m}") for m in range(MATS)]
        setup_pool, setup_exp, setup_dve = sem("setup_pool"), sem("setup_exp"), sem("setup_dve")
        conv_done = sem("conv_done")
        conv_taken = sem("conv_taken")
        u_done = sem("u_done")
        xdbl_done = sem("xdbl_done")
        dt_rows_done = sem("dt_rows_done")
        rows_hi_done = sem("rows_hi_done")
        rows_done = sem("rows_done")
        dtp_done = sem("dtp_done")
        abs_done = sem("abs_done")
        step_exp_done = sem("step_exp_done")
        step_w_done = sem("step_w_done")
        ln_done = sem("ln_done")
        delta_done = sem("delta_done")
        du_done = sem("du_done")
        z_done = sem("z_done")
        tanh_z_done = sem("tanh_z_done")
        gate2_done = sem("gate2_done")
        acc_ready = sem("acc_ready")
        yg_done = sem("yg_done")
        yt_done = sem("yt_done")
        x2_done = sem("x2_done")
        x2t_done = sem("x2t_done")
        x2_s_done = sem("x2_s_done")
        x2_hi_done = sem("x2_hi_done")
        x2_lo_done = sem("x2_lo_done")
        logits_done = sem("logits_done")
        shifted = sem("shifted")
        exp_done = sem("exp_done")
        out_stored = sem("out_stored")
        pre_link = sem("pre_link")
        post_link = sem("post_link")
        b_done = sem("b_done")
        c_done = sem("c_done")
        decay_done = sem("decay_done")
        drive_done = sem("drive_done")
        scan_done = sem("scan_done")
        part_done = sem("part_done")
        sum_done = sem("sum_done")
        gu_done = sem("gu_done")
        tanh_done = sem("tanh_done")
        gated_done = sem("gated_done")
        hid_done = sem("hid_done")
        hid_hi_done = sem("hid_hi_done")
        hid_lo_done = sem("hid_lo_done")
        down_done = sem("down_done")
        w_hi_done = sem("w_hi_done")
        split_done = sem("split_done")
        y_taken = sem("y_taken")

        block = stack.enter_context(nc.Block())

        def split_job(r, last):
            at = r % IC
            if at == IC - 1 and last < 1:
                return 2, GATE
            if at < 2 and last < 2:
                return 1, UP + at
            return None

        @block.sync
        def _(sp):
            x_tiles = x.rearrange("b (t p) h -> p b t h", p=P)
            out_tiles = out.rearrange("b (t p) h -> p b t h", p=P)
            pad = DC - 1
            sp.dma_start(par[:, :], params).then_inc(par_in, 16)
            sp.dma_start(dtw[:, :], dt_w).then_inc(par_in, 16)
            sp.dma_start(ctx_sb[:, 0:GB, pad:], ctx_t[:, 0:GB, :]).then_inc(x0_in, 16)
            sp.dma_start(x_sb[:, 0:GB].rearrange("p b t h -> p (b t) h"),
                         x_tiles[:, 0:GB].rearrange("p b t h -> p (b t) h")).then_inc(x0_in, 16)
            sp.dma_start(ctx_sb[:, GB:B, pad:], ctx_t[:, GB:B, :]).then_inc(rest_in, 16)
            sp.dma_start(x_sb[:, GB:B].rearrange("p b t h -> p (b t) h"),
                         x_tiles[:, GB:B].rearrange("p b t h -> p (b t) h")).then_inc(rest_in, 16)

            def load(n, e, m):
                sp.dma_start(w_raw[m][:, :], weights[e, m]).then_inc(w_in[m], 16)

            for m in range(MATS):
                load(0, 0, m)
            for first, end in ((1, X), (X, G * X)):
                with sp.Fori(first, end) as n:
                    for m in range(MATS):
                        sp.wait_ge(split_done, (n - 1) * MATS + m + 1)
                        load(n, n if first == 1 else n - X, m)
            for g in range(G):
                sp.wait_ge(y_taken, (g + 1) * X + 1)
                for b in range(g * GB, (g + 1) * GB):
                    sp.dma_start(out_tiles[:, b], x_sb[:, b]).then_inc(out_stored, 16)
            sp.wait_ge(out_stored, 16 * B)

        @block.tensor
        def _(pe):
            def convolve(g):
                if g > 0:
                    pe.wait_ge(conv_taken, g)
                for k in range(KH):
                    bank = ps_y[k][:, :, :].rearrange("p t h -> p (t h)")
                    for b in range(GB):
                        for j in range(DC):
                            mm = nc.tensor.matmul(bank[:, b * L:(b + 1) * L], in_wk[:, j, k * P:(k + 1) * P],
                                                  ctx_sb[:, g * GB + b, j:j + L], start=(b == 0 and j == 0),
                                                  stop=(j == DC - 1), skip_group_check=True)
                mm.then_inc(conv_done, 1)

            def x_proj(g):
                pe.wait_ge(u_done, g + 1)
                if g > 0:
                    pe.wait_ge(dt_rows_done, g)
                    pe.wait_ge(rows_done, g)
                for k in range(KH):
                    nc.tensor.matmul(ps_up[1][0:DR, :], xp_w[:, k, 0:DR], u[g][:, k, :],
                                     start=(k == 0), stop=(k == KH - 1))
                for k in range(KH):
                    mm = nc.tensor.matmul(ps_up[0][0:PARTS * BC, :], xp_w[:, k, DR:DR + PARTS * BC], u[g][:, k, :],
                                          start=(k == 0), stop=(k == KH - 1))
                mm.then_inc(xdbl_done, 1)

            def dt_proj(g):
                pe.wait_ge(dt_rows_done, g + 1)
                if g > 0:
                    pe.wait_ge(abs_done, g)
                for k in range(KH):
                    mm = nc.tensor.matmul(ps_gate[k][:, :], dtw[:, k * P:(k + 1) * P], dt_rows[:, :],
                                          start=True, stop=True)
                mm.then_inc(dtp_done, 1)

            def spread(g, n):
                v = g * UNITS + n * KH
                for bank, first, used, done in ((ps_b, 0, drive_done, b_done), (ps_c, NS, part_done, c_done)):
                    pe.wait_ge(used, v + 2)
                    nc.tensor.matmul(bank[:, :], sel[:, bass.ds(n + first, 1)].to_broadcast([PARTS * BC, P]),
                                     rows[g][:, :], start=True, stop=True).then_inc(done, 1)

            def spreads(g, first, end):
                with pe.Fori(first, end) as n:
                    spread(g, n)

            def transpose_y(g):
                pe.wait_ge(yg_done, g + 1)
                for b in range(GB):
                    bank = ps_m[b][:, :].rearrange("p (t h) -> p t h", t=TL)
                    for t in range(TL):
                        for k in range(KH):
                            at = b * L + t * P
                            mm = nc.tensor.transpose(bank[:, t, k * P:(k + 1) * P], yg[:, k, at:at + P], ident)
                mm.then_inc(yt_done, 1)

            def transpose_x2(g):
                pe.wait_ge(x2_done, g + 1)
                for k in range(KH):
                    for t in range(TT):
                        mm = nc.tensor.transpose(ps_m[k][:, t * P:(t + 1) * P], x2[:, t, k * P:(k + 1) * P], ident)
                mm.then_inc(x2t_done, 1)

            def logits(g):
                pe.wait_ge(x2_s_done, g + 1)
                for t in range(TT):
                    for k in range(KH):
                        mm = nc.tensor.matmul(ps_b[:, t * E:(t + 1) * E], x2_s[:, k, t * P:(t + 1) * P],
                                              wg[:, k, :], start=(t == 0 and k == 0), stop=(k == KH - 1),
                                              skip_group_check=True)
                mm.then_inc(logits_done, 1)

            def gate_up(g, p, r):
                c, at, i = g * SLOTS + p * PAIR + r, r % IC, (r // IC + g) % 2
                if at == 0:
                    pe.wait_ge(split_done, expert(g, p, r) * MATS + UP + 1)
                pe.wait_ge(hid_done, c + 1)
                for bank, m in ((ps_gate[r % 2], GATE), (ps_up[r % 2], UP)):
                    todo = [(w, act, k) for w, act in ((w_hi, x2_hi), (w_hi, x2_lo), (w_lo, x2_hi)) for k in range(KH)]
                    for n, (w, act, k) in enumerate(todo):
                        col = k * I + at * P
                        mm = nc.tensor.matmul(bank[:, :], w[i][m][:, col:col + P], act[g][:, k, :],
                                              start=(n == 0), stop=(n == len(todo) - 1))
                mm.then_inc(gu_done, 1)

            def down(g, p, r):
                c, at, i = g * SLOTS + p * PAIR + r, r % IC, (r // IC + g) % 2
                if at == 0:
                    pe.wait_ge(split_done, expert(g, p, r) * MATS + DOWN + 1)
                    pe.wait_ge(y_taken, expert(g, p, r) + 1)
                pe.wait_ge(hid_lo_done, c + 3)
                for t in range(TT):
                    for n, (h, w) in enumerate(((hid_hi, w_hi), (hid_hi, w_lo), (hid_lo, w_hi))):
                        mm = nc.tensor.matmul(ps_y[t // 2][:, t % 2, :], h[r % 2][:, t * P:(t + 1) * P],
                                              w[i][DOWN][:, at * H:(at + 1) * H],
                                              start=(at == 0 and n == 0 and t % 2 == 0),
                                              stop=(at == IC - 1 and n == 2), skip_group_check=True)
                mm.then_inc(down_done, 1)

            def expert(g, p, r):
                return g * X + p * 2 + r // IC

            def pair(g, p):
                for r in range(PAIR):
                    if g == 0 and r % KH == 0:
                        spread(1, p * (PAIR // KH) + r // KH)
                    gate_up(g, p, r + 2)
                    down(g, p, r)

            pe.wait_ge(par_in, 32)
            pe.wait_ge(x0_in, 32)
            pe.wait_ge(setup_dve, 4)
            pe.wait_ge(setup_pool, 5)
            convolve(0)
            pe.wait_ge(rest_in, 32)
            x_proj(0)
            dt_proj(0)
            convolve(1)
            pe.wait_ge(rows_done, 1)
            spreads(0, 0, CUTS[0])
            x_proj(1)
            spreads(0, CUTS[0], CUTS[1])
            dt_proj(1)
            spreads(0, CUTS[1], NS)
            transpose_y(0)
            transpose_x2(0)
            logits(0)
            for g in range(G):
                if g == 0:
                    pe.wait_ge(delta_done, G)
                    pe.wait_ge(rows_done, G)
                    pe.wait_ge(shifted, 1)
                pe.wait_ge(x2_lo_done, g + 1)
                gate_up(g, 0, 0)
                gate_up(g, 0, 1)
                pair(g, 0)
                with pe.Fori(1, E // 2) as p:
                    pair(g, p)
                gate_up(g, E // 2, 2)
                down(g, E // 2, 0)
                if g == 0:
                    transpose_y(1)
                gate_up(g, E // 2, 3)
                for r in range(1, IC):
                    down(g, E // 2, r)
                if g == 0:
                    transpose_x2(1)
                    logits(1)

        @block.scalar
        def _(act):
            def take_conv(g):
                act.wait_ge(conv_done, g + 1)
                if g > 0:
                    act.wait_ge(delta_done, g)
                for k in range(KH):
                    bank = ps_y[k][:, :, :].rearrange("p t h -> p (t h)")
                    nc.scalar.activation(conv_h[:, k, :], bank, ACT.Identity, bias=convb[:, k:k + 1], scale=0.5)
                    ins = nc.scalar.activation(tanh_u[:, k, :], bank, ACT.Tanh, bias=convb[:, k:k + 1], scale=0.5)
                ins.then_inc(conv_taken, 1)

            def take_z(g):
                act.wait_ge(z_done, g + 1)
                nc.scalar.activation(tanh_z[:, :, :], z[:, :, :], ACT.Tanh, scale=0.5).then_inc(tanh_z_done, 1)

            def take_rows(g):
                act.wait_ge(xdbl_done, g + 1)
                nc.scalar.copy(dt_rows[:, :], ps_up[1][0:DR, :]).then_inc(dt_rows_done, 1)
                nc.scalar.copy(rows[g][:, :], ps_up[0][0:PARTS * BC, :]).then_inc(rows_hi_done, 1)

            def take_step(g):
                act.wait_ge(dtp_done, g + 1)
                act.wait_ge(u_done, g + 1)
                for k in range(KH):
                    nc.scalar.activation(step_v[:, k, :], ps_gate[k][:, :], ACT.Identity, bias=dt_b[:, k:k + 1])
                    ins = nc.scalar.activation(step_abs[:, k, :], ps_gate[k][:, :], ACT.Abs, bias=dt_b[:, k:k + 1])
                ins.then_inc(abs_done, 1)
                act.wait_ge(abs_done, g + 1)
                nc.scalar.activation(step_e[:, :, :], step_abs[:, :, :], ACT.Exp, scale=-1.0).then_inc(step_exp_done, 1)
                act.wait_ge(step_w_done, g + 1)
                nc.scalar.activation(step_ln[:, :, :], step_w[:, :, :], ACT.Ln).then_inc(ln_done, 1)

            def unit_decay(g, n, k):
                v = g * UNITS + n * KH + k
                act.wait_ge(scan_done, v + 1)
                dst = decay[k][:, :, 1:L]
                nc.scalar.activation(dst, delta[g][:, k, :].rearrange("p (b l) -> p b l", b=GB)[:, :, 1:L], ACT.Exp,
                                     scale=a_neg[:, k, bass.ds(n, 1)]).then_inc(decay_done, 1)

            def decays(g, first, end):
                act.wait_ge(delta_done, g + 1)
                with act.Fori(first, end) as n:
                    for k in range(KH):
                        unit_decay(g, n, k)

            def take_x2(g):
                act.wait_ge(x2t_done, g + 1)
                for k in range(KH):
                    ins = nc.scalar.copy(x2_s[:, k, :], ps_m[k][:, :])
                ins.then_inc(x2_s_done, 1)
                act.wait_ge(x2_s_done, g + 1)
                nc.scalar.copy(x2_hi[g][:, :, :], x2_s[:, :, :]).then_inc(x2_hi_done, 1)

            def router_exp(g):
                act.wait_ge(shifted, g + 1)
                nc.scalar.activation(prob[:, :, :], logit[:, :, :], ACT.Exp).then_inc(exp_done, 1)

            def split_hi(n, i, m):
                act.wait_ge(w_in[m], (n + 1) * 16)
                if not (isinstance(n, int) and n < 2):
                    if m == DOWN:
                        act.wait_ge(down_done, (n - 1) * IC + 2)
                    else:
                        act.wait_ge(gu_done, (n - 1) * IC)
                nc.scalar.copy(w_hi[i][m][:, :], w_raw[m][:, :]).then_inc(w_hi_done, 1)

            def gate_tanh(g, q, r):
                act.wait_ge(gu_done, g * SLOTS + q + 1)
                nc.scalar.activation(tanh_g[r % 2][:, :], ps_gate[r % 2][:, :], ACT.Tanh, scale=0.5).then_inc(tanh_done, 1)

            def round_hid(g, q, r):
                c = g * SLOTS + q
                act.wait_ge(hid_done, c + 3)
                act.wait_ge(down_done, c + 1)
                nc.scalar.copy(hid_hi[r % 2][:, :], hid[r % 2][:, :]).then_inc(hid_hi_done, 1)

            def slot(g, p, r, last=0, ends=False):
                gate_tanh(g, p * PAIR + r, r)
                if g == 0 and not ends:
                    unit_decay(1, p * (PAIR // KH) + r // KH, r % KH)
                round_hid(g, p * PAIR + r, r)
                if split_job(r, last):
                    ahead, m = split_job(r, last)
                    split_hi(g * X + p * 2 + r // IC + ahead, (r // IC + ahead + g) % 2, m)

            act.wait_ge(par_in, 32)
            nc.scalar.activation(a_neg[:, :, :], par[:, C_ALOG:C_D].rearrange("p (k n) -> p k n", k=KH),
                                 ACT.Exp).then_inc(setup_exp, 1)
            act.wait_ge(setup_dve, 4)
            act.wait_ge(setup_pool, 5)
            take_conv(0)
            take_z(0)
            for m in range(MATS):
                split_hi(0, 0, m)
            take_rows(0)
            take_step(0)
            split_hi(1, 1, GATE)
            decays(0, 0, CUTS[0])
            take_conv(1)
            take_z(1)
            decays(0, CUTS[0], CUTS[1])
            take_rows(1)
            decays(0, CUTS[1], CUTS[2])
            take_step(1)
            decays(0, CUTS[2], NS)
            take_x2(0)
            router_exp(0)
            act.wait_ge(delta_done, G)
            for g in range(G):
                for r in range(PAIR):
                    slot(g, 0, r)
                full = E // 2 if g == 0 else E // 2 - 1
                with act.Fori(1, full) as p:
                    for r in range(PAIR):
                        slot(g, p, r)
                if g == 1:
                    for r in range(PAIR):
                        slot(g, full, r, last=r // IC)
                for r in range(IC):
                    slot(g, E // 2, r, last=0 if g == 0 else 2, ends=True)
                if g == 0:
                    take_x2(1)
                    router_exp(1)

        @block.gpsimd
        def _(pool):
            nc.gpsimd.memset(ctx_sb[:, :, 0:DC - 1], 0.0).then_inc(setup_pool, 1)
            for i in range(2):
                nc.gpsimd.memset(decay[i][:, :, 0:1], 0.0).then_inc(setup_pool, 1)
            pool.wait_ge(par_in, 32)
            nc.gpsimd.tensor_copy(sel[:, :], par[0:PARTS * BC, C_SEL:C_CONVB]).then_inc(setup_pool, 1)
            nc.gpsimd.tensor_tensor(in_wk[:, :, :], taps, in_w.unsqueeze(1).to_broadcast([P, DC, H]),
                                    ALU.mult).then_inc(setup_pool, 1)
            pool.sem_inc(sum_done, 2)
            pool.sem_inc(hid_lo_done, 2)

            def start_sum(g):
                if g > 0:
                    pool.wait_ge(yg_done, g)
                pool.wait_ge(u_done, g + 1)
                nc.gpsimd.tensor_tensor(y_acc[:, :, :], u[g][:, :, :], d_skip.unsqueeze(2).to_broadcast([P, KH, T]),
                                        ALU.mult).then_inc(acc_ready, 1)
                pool.wait_ge(acc_ready, g + 1)

            def add_unit(g, n, k):
                v = g * UNITS + n * KH + k
                pool.wait_ge(part_done, v + 3)
                pool.wait_ge(sum_done, v + 1)
                nc.gpsimd.tensor_tensor(y_acc[:, k, :], y_acc[:, k, :], part[k][:, :], ALU.add).then_inc(sum_done, 1)

            def sums(g, first, end):
                with pool.Fori(first, end) as n:
                    for k in range(KH):
                        add_unit(g, n, k)

            def split_lo(n, i, m):
                pool.wait_ge(w_hi_done, n * MATS + m + 1)
                nc.gpsimd.tensor_tensor(w_lo[i][m][:, :], w_raw[m][:, :], w_hi[i][m][:, :].bitcast(F32),
                                        ALU.subtract).then_inc(split_done, 1)

            def rest_hid(g, q, r):
                pool.wait_ge(hid_hi_done, g * SLOTS + q + 1)
                nc.gpsimd.tensor_tensor(hid_lo[r % 2][:, :], hid[r % 2][:, :], hid_hi[r % 2][:, :].bitcast(F32),
                                        ALU.subtract).then_inc(hid_lo_done, 1)

            def rest_x2(g):
                pool.wait_ge(x2_hi_done, g + 1)
                nc.gpsimd.tensor_tensor(x2_lo[g][:, :, :], x2_s[:, :, :], x2_hi[g][:, :, :].bitcast(F32),
                                        ALU.subtract).then_inc(x2_lo_done, 1)

            def slot(g, p, r, last=0, ends=False):
                rest_hid(g, p * PAIR + r, r)
                if split_job(r, last):
                    ahead, m = split_job(r, last)
                    split_lo(g * X + p * 2 + r // IC + ahead, (r // IC + ahead + g) % 2, m)
                if g == 0 and not ends:
                    add_unit(1, p * (PAIR // KH) + r // KH, r % KH)

            start_sum(0)
            for n, m in ((0, GATE), (0, UP), (0, DOWN), (1, GATE)):
                split_lo(n, n, m)
            sums(0, 0, NS)
            start_sum(1)
            rest_x2(0)
            for g in range(G):
                for r in range(PAIR):
                    slot(g, 0, r)
                full = E // 2 if g == 0 else E // 2 - 1
                with pool.Fori(1, full) as p:
                    for r in range(PAIR):
                        slot(g, p, r)
                if g == 1:
                    for r in range(PAIR):
                        slot(g, full, r, last=r // IC)
                for r in range(IC):
                    slot(g, E // 2, r, last=0 if g == 0 else 2, ends=True)
                if g == 0:
                    rest_x2(1)

        @block.vector
        def _(dve):
            links = {}

            def link(ins, chain):
                links[chain.name] = links.get(chain.name, 0) + 1
                ins.then_inc(chain, 1)
                dve.wait_ge(chain, links[chain.name])

            def pre(ins):
                link(ins, pre_link)

            def post(ins):
                link(ins, post_link)

            def rsqrt(step):
                y = yi[:, :].bitcast(F32)
                step(nc.vector.tensor_scalar(ve[:, :], mv[:, :, 1], EPS, None, ALU.add))
                step(nc.vector.tensor_scalar(yi[:, :], ve[:, :].bitcast(I32), 1, None, ALU.logical_shift_right))
                step(nc.vector.tensor_scalar(yi[:, :], yi[:, :], -1.0, float(SEED), ALU.mult, ALU.add))
                for _ in range(3):
                    step(nc.vector.scalar_tensor_tensor(out=nr[:, :], in0=y, scalar=-0.5, in1=y, op0=ALU.mult,
                                                        op1=ALU.mult))
                    step(nc.vector.tensor_tensor(nr[:, :], nr[:, :], ve[:, :], ALU.mult))
                    step(nc.vector.scalar_tensor_tensor(out=y, in0=nr[:, :], scalar=1.5, in1=y, op0=ALU.add,
                                                        op1=ALU.mult))
                return y

            def norm(g, step, dst):
                for t in range(TT):
                    ins = nc.vector.bn_stats(stats[:, t, :], x_sb[:, g * GB + t // TL, t % TL, :])
                step(ins)
                for t in range(TT):
                    ins = nc.vector.bn_aggr(mv[:, t, :], stats[:, t, :])
                step(ins)
                y = rsqrt(step)
                for t in range(TT):
                    ins = nc.vector.tensor_scalar(dst(t), x_sb[:, g * GB + t // TL, t % TL, :], mv[:, t, 0:1],
                                                  y[:, t:t + 1], ALU.subtract, ALU.mult)
                return ins

            def pre_norm(g):
                if g > 0:
                    dve.wait_ge(gate2_done, g)
                norm(g, pre, lambda t: z[:, t % TL, (t // TL) * L:(t // TL + 1) * L]).then_inc(z_done, 1)

            def pre_u(g):
                dve.wait_ge(conv_taken, g + 1)
                nc.vector.scalar_tensor_tensor(out=u[g][:, :, :], in0=tanh_u[:, :, :], scalar=1.0,
                                               in1=conv_h[:, :, :], op0=ALU.add, op1=ALU.mult).then_inc(u_done, 1)

            def pre_gate(g):
                dve.wait_ge(tanh_z_done, g + 1)
                nc.vector.scalar_tensor_tensor(out=gate2[g][:, :, :], in0=tanh_z[:, :, :], scalar=1.0,
                                               in1=z[:, :, :], op0=ALU.add, op1=ALU.mult).then_inc(gate2_done, 1)

            def pre_rows(g):
                a, b, c = (slice(n * BC, (n + 1) * BC) for n in range(PARTS))
                dve.wait_ge(rows_hi_done, g + 1)
                nc.vector.tensor_tensor(row_rest[c, :], ps_up[0][c, :], rows[g][c, :], ALU.subtract)
                pre(nc.vector.tensor_tensor(rows[g][b, :], ps_up[0][b, :], rows[g][b, :], ALU.subtract))
                pre(nc.vector.tensor_copy(row_mid[c, :], row_rest[c, :]))
                nc.vector.tensor_tensor(rows[g][c, :], row_rest[c, :], row_mid[c, :],
                                        ALU.subtract).then_inc(rows_done, 1)

            def pre_step(g):
                dve.wait_ge(step_exp_done, g + 1)
                nc.vector.tensor_scalar(step_w[:, :, :], step_e[:, :, :], 1.0, None, ALU.add).then_inc(step_w_done, 1)
                dve.wait_ge(step_w_done, g + 1)
                pre(nc.vector.scalar_tensor_tensor(out=step_e[:, :, :], in0=step_w[:, :, :], scalar=-1.0,
                                                   in1=step_e[:, :, :], op0=ALU.add, op1=ALU.subtract))
                dve.wait_ge(ln_done, g + 1)
                pre(nc.vector.tensor_tensor(step_e[:, :, :], step_ln[:, :, :], step_e[:, :, :], ALU.subtract))
                nc.vector.scalar_tensor_tensor(out=delta[g][:, :, :], in0=step_v[:, :, :], scalar=0.0,
                                               in1=step_e[:, :, :], op0=ALU.max, op1=ALU.add).then_inc(delta_done, 1)
                dve.wait_ge(delta_done, g + 1)
                nc.vector.tensor_tensor(du[g][:, :, :], delta[g][:, :, :], u[g][:, :, :], ALU.mult).then_inc(du_done, 1)

            def unit_drive(g, n, k):
                v = g * UNITS + n * KH + k
                dve.wait_ge(b_done, g * NS + n + 1)
                dve.wait_ge(scan_done, v + 1)
                nc.vector.tensor_tensor(drive[k][:, :], du[g][:, k, :], ps_b[:, :], ALU.mult).then_inc(drive_done, 1)

            def unit_scan(g, n, k):
                v = g * UNITS + n * KH + k
                dve.wait_ge(drive_done, v + 3)
                dve.wait_ge(decay_done, v + 1)
                dve.wait_ge(part_done, v + 1)
                nc.vector.tensor_tensor_scan(state[k][:, :], decay[k][:, :, :].rearrange("p b l -> p (b l)"),
                                             drive[k][:, :], 0.0, ALU.mult, ALU.add).then_inc(scan_done, 1)

            def unit_part(g, n, k):
                v = g * UNITS + n * KH + k
                dve.wait_ge(c_done, g * NS + n + 1)
                dve.wait_ge(scan_done, v + 3)
                dve.wait_ge(sum_done, v + 1)
                nc.vector.tensor_tensor(part[k][:, :], state[k][:, :], ps_c[:, :], ALU.mult).then_inc(part_done, 1)

            def units(g, first, end):
                dve.wait_ge(du_done, g + 1)
                with dve.Fori(first, end) as n:
                    for step in (unit_drive, unit_scan, unit_part):
                        for k in range(KH):
                            step(g, n, k)

            def post_gate(g):
                dve.wait_ge(sum_done, (g + 1) * UNITS + 2)
                nc.vector.scalar_tensor_tensor(out=yg[:, :, :], in0=y_acc[:, :, :], scalar=0.5, in1=gate2[g][:, :, :],
                                               op0=ALU.mult, op1=ALU.mult).then_inc(yg_done, 1)

            def post_norm(g):
                dve.wait_ge(yt_done, g + 1)
                for b in range(GB):
                    xb = x_sb[:, g * GB + b].rearrange("p t h -> p (t h)")
                    ins = nc.vector.tensor_tensor(xb, xb, ps_m[b][:, :], ALU.add)
                post(ins)
                norm(g, post, lambda t: x2[:, t, :]).then_inc(x2_done, 1)

            def route(g):
                def wide(ap):
                    return ap.unsqueeze(2).to_broadcast([P, TT, E])

                ranks = rank.unsqueeze(1).to_broadcast([P, TT, E])
                top, total, first, second, mark, share = (small[:, n, :] for n in range(6))
                dve.wait_ge(logits_done, g + 1)
                lg = ps_b[:, 0:TT * E].rearrange("p (t e) -> p t e", t=TT)
                post(nc.vector.tensor_reduce(top, lg, AX_X, ALU.max))
                nc.vector.tensor_tensor(logit[:, :, :], lg, wide(top), ALU.subtract).then_inc(shifted, 1)
                dve.wait_ge(exp_done, g + 1)
                post(nc.vector.tensor_reduce(total, prob[:, :, :], AX_X, ALU.add))
                post(nc.vector.reciprocal(total, total))
                post(nc.vector.tensor_tensor(prob[:, :, :], prob[:, :, :], wide(total), ALU.mult))
                post(nc.vector.tensor_reduce(first, prob[:, :, :], AX_X, ALU.max))
                post(nc.vector.tensor_tensor(pick[:, :, :], prob[:, :, :], wide(first), ALU.is_equal))
                post(nc.vector.tensor_tensor(pick[:, :, :], pick[:, :, :], ranks, ALU.mult))
                post(nc.vector.tensor_reduce(mark, pick[:, :, :], AX_X, ALU.max))
                post(nc.vector.tensor_tensor(pick[:, :, :], ranks, wide(mark), ALU.is_equal))
                post(nc.vector.scalar_tensor_tensor(out=rest[:, :, :], in0=pick[:, :, :], scalar=-2.0,
                                                    in1=prob[:, :, :], op0=ALU.mult, op1=ALU.add))
                post(nc.vector.tensor_reduce(second, rest[:, :, :], AX_X, ALU.max))
                post(nc.vector.tensor_tensor(pick2[:, :, :], rest[:, :, :], wide(second), ALU.is_equal))
                post(nc.vector.tensor_tensor(pick2[:, :, :], pick2[:, :, :], ranks, ALU.mult))
                post(nc.vector.tensor_reduce(mark, pick2[:, :, :], AX_X, ALU.max))
                post(nc.vector.tensor_tensor(pick2[:, :, :], ranks, wide(mark), ALU.is_equal))
                post(nc.vector.tensor_tensor(share, first, second, ALU.add))
                post(nc.vector.tensor_scalar(share, share, 2.0, None, ALU.mult))
                post(nc.vector.reciprocal(share, share))
                post(nc.vector.tensor_tensor(pick[:, :, :], pick[:, :, :], pick2[:, :, :], ALU.add))
                post(nc.vector.tensor_tensor(pick[:, :, :], pick[:, :, :], prob[:, :, :], ALU.mult))
                post(nc.vector.tensor_tensor(wts[:, :, :], pick[:, :, :], wide(share), ALU.mult))

            def gate_mul(g, q, r):
                dve.wait_ge(tanh_done, g * SLOTS + q + 1)
                dve.wait_ge(hid_done, g * SLOTS + q + 2)
                nc.vector.scalar_tensor_tensor(out=gated[:, :], in0=tanh_g[r % 2][:, :], scalar=1.0,
                                               in1=ps_gate[r % 2][:, :], op0=ALU.add, op1=ALU.mult).then_inc(gated_done, 1)

            def up_mul(g, q, r):
                dve.wait_ge(gated_done, g * SLOTS + q + 1)
                dve.wait_ge(hid_lo_done, g * SLOTS + q + 1)
                nc.vector.tensor_tensor(hid[r % 2][:, :], gated[:, :], ps_up[r % 2][:, :], ALU.mult).then_inc(hid_done, 1)

            def add_expert(g, e):
                dve.wait_ge(down_done, g * SLOTS + e * IC + IC + 2)
                for t in range(TT):
                    weight = 0.5 if isinstance(e, int) and e == E else wts[:, t, bass.ds(e, 1)]
                    xt = x_sb[:, g * GB + t // TL, t % TL, :]
                    ins = nc.vector.scalar_tensor_tensor(out=xt, in0=ps_y[t // 2][:, t % 2, :], scalar=weight,
                                                         in1=xt, op0=ALU.mult, op1=ALU.add)
                ins.then_inc(y_taken, 1)

            def slot(g, p, r, ends=False):
                unit = (1, p * (PAIR // KH) + r // KH, r % KH) if g == 0 and not ends else None
                gate_mul(g, p * PAIR + r, r)
                up_mul(g, p * PAIR + r, r)
                if r % IC == 1 and not (isinstance(p, int) and p == 0 and r == 1):
                    add_expert(g, p * 2 + r // IC - 1)
                if unit:
                    unit_drive(*unit)
                    unit_scan(*unit)
                    unit_part(*unit)

            dve.wait_ge(par_in, 32)
            nc.vector.tensor_scalar(convb[:, :], par[:, C_CONVB:C_DTB], 0.5, None, ALU.mult).then_inc(setup_dve, 1)
            dve.wait_ge(setup_exp, 1)
            nc.vector.tensor_scalar(a_neg[:, :, :], a_neg[:, :, :], -1.0, None, ALU.mult).then_inc(setup_dve, 1)
            for s, n in ((hid_done, 2), (drive_done, 2), (down_done, 2), (scan_done, 2), (part_done, 2), (y_taken, 1), (setup_dve, 2)):
                dve.sem_inc(s, n)
            dve.wait_ge(x0_in, 32)
            pre_norm(0)
            pre_u(0)
            pre_gate(0)
            dve.wait_ge(rest_in, 32)
            pre_norm(1)
            pre_rows(0)
            pre_step(0)
            units(0, 0, CUTS[0])
            pre_u(1)
            pre_gate(1)
            units(0, CUTS[0], CUTS[1])
            pre_rows(1)
            units(0, CUTS[1], CUTS[2])
            pre_step(1)
            units(0, CUTS[2], NS)
            post_gate(0)
            post_norm(0)
            route(0)
            dve.wait_ge(du_done, G)
            for g in range(G):
                for r in range(PAIR):
                    slot(g, 0, r)
                with dve.Fori(1, E // 2) as p:
                    for r in range(PAIR):
                        slot(g, p, r)
                for r in range(IC):
                    slot(g, E // 2, r, ends=True)
                    if g == 0 and r == 0:
                        post_gate(1)
                if g == 0:
                    post_norm(1)
                add_expert(g, E)
                if g == 0:
                    route(1)


def kernel(x, ctx_1024, L0_xattn_in_proj_w, L0_xattn_conv_w, L0_xattn_conv_b, L0_xattn_x_proj_w,
           L0_xattn_dt_proj_w, L0_xattn_dt_proj_b, L0_xattn_A_log, L0_xattn_D, L0_ffn_wg, L0_ffn_gate_w,
           L0_ffn_up_w, L0_ffn_down_w, L0_ffn_shared_gate_w, L0_ffn_shared_up_w, L0_ffn_shared_down_w):
    import numpy as np
    import concourse.bacc as bacc
    from concourse.bass_utils import run_bass_kernel_spmd

    def halves(a):
        a = np.asarray(a).reshape(-1, P, int(np.prod(np.shape(a)[1:], dtype=int)))
        return a.transpose(1, 0, 2).reshape(P, -1)

    xp = np.asarray(L0_xattn_x_proj_w).T
    xp = np.concatenate([xp[:, :DR]] + [xp[:, DR:]] * PARTS, axis=1)
    sel = np.zeros((P, BC), np.float32)
    sel[:PARTS * BC] = np.tile(np.eye(BC, dtype=np.float32), (PARTS, 1))
    params = np.concatenate([
        np.eye(P, dtype=np.float32),
        np.tile(np.arange(E, 0, -1, dtype=np.float32), (P, 1)), sel,
        halves(L0_xattn_conv_b), halves(L0_xattn_dt_proj_b), halves(L0_xattn_A_log),
        halves(L0_xattn_D), np.asarray(L0_xattn_in_proj_w).T, halves(xp),
        halves(np.asarray(L0_ffn_wg).T),
        np.tile(np.asarray(L0_xattn_conv_w).T.reshape(1, -1), (P, 1))], axis=1)
    gate = np.concatenate([np.asarray(L0_ffn_gate_w), np.asarray(L0_ffn_shared_gate_w)[None]])
    up = np.concatenate([np.asarray(L0_ffn_up_w), np.asarray(L0_ffn_shared_up_w)[None]])
    down = np.concatenate([np.asarray(L0_ffn_down_w), np.asarray(L0_ffn_shared_down_w)[None]])
    weights = np.stack([np.stack([halves(gate[e]), halves(up[e]), halves(down[e])]) for e in range(X)])
    arrays = {
        "x": np.ascontiguousarray(x),
        "ctx_t": np.ascontiguousarray(np.asarray(ctx_1024).transpose(2, 0, 1)),
        "params": np.ascontiguousarray(params),
        "dt_w": np.ascontiguousarray(np.asarray(L0_xattn_dt_proj_w).T),
        "weights": np.ascontiguousarray(weights),
    }
    nc = bacc.Bacc("TRN2", target_bir_lowering=False, num_devices=1)
    args = [nc.dram_tensor(name, a.shape, mybir.dt.from_np(a.dtype), kind="ExternalInput").ap()
            for name, a in arrays.items()]
    args.append(nc.dram_tensor("out", (B, L, H), F32, kind="ExternalOutput").ap())
    build(nc, *args)
    result = run_bass_kernel_spmd(nc, [arrays], core_ids=[0])
    return result.results[0]["out"]
```

```python
from contextlib import ExitStack

import concourse.bass as bass
from concourse import mybir

F32 = mybir.dt.float32
F32R = mybir.dt.float32r
BF16 = mybir.dt.bfloat16
I32 = mybir.dt.int32
ALU = mybir.AluOpType
ACT = mybir.ActivationFunctionType
AX_X = mybir.AxisListType.X

P = 128
B = 4
L = 256
TL = L // P
G = 2
GB = B // G
T = GB * L
TT = T // P
DM = 128
H = 256
KH = H // P
NS = 16
DR = 8
DC = 4
I = 512
E = 8
EPS = 1e-5
IC = I // P
X = E + 1
SLOTS = X * IC
UNITS = NS * KH
PAIR = 2 * IC
MATS = 3
MAT_COLS = KH * I
GATE, UP, DOWN = range(MATS)
SUMS_AHEAD = (2, 1)
BC = 2 * NS
PARTS = 3
XP = PARTS * BC + DR
SEED = 0x5F3759DF
CUTS = (2, 8, 14)
STATE_XP = CUTS[0] + 1
STATE_DT = CUTS[1]
EARLY = 3
LATE = KH
PAIRS = E // 2
assert UNITS == (E // 2) * PAIR and (I // P) * H == MAT_COLS

C_INW = 0
C_TAPS = C_INW + H
C_IDENT = C_TAPS + DC * H
C_RANK = C_IDENT + P
C_SEL = C_RANK + E
C_CONVB = C_SEL + BC
C_DTB = C_CONVB + KH
C_ALOG = C_DTB + KH
C_D = C_ALOG + KH * NS
C_XPW = C_D + KH
C_WG = C_XPW + KH * XP
C_END = C_WG + KH * E


def build(nc, x, ctx_t, params, dt_w, weights, out):
    with ExitStack() as stack:
        def sb(name, shape, dt=F32):
            return stack.enter_context(nc.sbuf_tensor(name, shape, dt))

        def ps(name, shape):
            return stack.enter_context(nc.psum_tensor(name, shape, F32))

        def sem(name):
            return stack.enter_context(nc.semaphore(name))

        w_raw = [sb(f"w_raw{m}", [P, MAT_COLS]) for m in range(MATS)]
        w_hi = [[sb(f"w_hi{i}{m}", [P, MAT_COLS], F32R) for m in range(MATS)] for i in range(2)]
        w_lo = [[sb(f"w_lo{i}{m}", [P, MAT_COLS], F32R) for m in range(MATS)] for i in range(2)]
        par = sb("par", [P, C_END])
        dtw = sb("dtw", [DR, H])
        x_sb = sb("x_sb", [P, B, TL, H])
        ctx_sb = sb("ctx_sb", [P, B, DC - 1 + L])
        sel = sb("sel", [PARTS * BC, BC], BF16)
        convb = sb("convb", [P, KH])
        a_neg = sb("a_neg", [P, KH, NS])
        bufs = [sb(f"buf{i}", [P, KH, T]) for i in range(4)]
        conv_h, tanh_u, z, tanh_z = bufs
        step_v, step_abs, step_e, step_w = bufs[0], bufs[1], sb("step_e", [P, KH, T]), bufs[1]
        step_ln = sb("step_ln", [P, KH, T])
        rows = [sb(f"rows{g}", [PARTS * BC, T], BF16) for g in range(G)]
        row_rest = sb("row_rest", [PARTS * BC, T])
        row_mid = sb("row_mid", [PARTS * BC, T], BF16)
        dt_rows = sb("dt_rows", [DR, T])
        u = [sb(f"u{g}", [P, KH, T]) for g in range(G)]
        delta = [sb(f"delta{g}", [P, KH, T]) for g in range(G)]
        du = [sb(f"du{g}", [P, KH, T]) for g in range(G)]
        gate2 = [sb(f"gate2{g}", [P, KH, T]) for g in range(G)]
        decay = [sb(f"decay{i}", [P, GB, L]) for i in range(2)]
        drive = [sb(f"drive{i}", [P, T]) for i in range(KH)]
        state = [sb(f"state{i}", [P, T]) for i in range(KH)]
        b_row = sb("b_row", [P, T])
        part = [sb(f"part{i}", [P, T]) for i in range(KH)]
        part_odd = sb("part_odd", [P, T])
        yg = sb("yg", [P, KH, T])
        x2 = yg[:, :, :].rearrange("p k t -> p (k t)").rearrange("p (t h) -> p t h", t=TT)
        x2_s = step_ln
        x2_hi = [sb(f"x2_hi{g}", [P, KH, T], F32R) for g in range(G)]
        x2_lo = [sb(f"x2_lo{g}", [P, KH, T], F32R) for g in range(G)]
        stats = sb("stats", [P, B * TL, 6])
        mv = sb("mv", [P, B * TL, 2])
        ve = sb("ve", [P, B * TL])
        yi = sb("yi", [P, B * TL], I32)
        nr = sb("nr", [P, B * TL])
        logit = sb("logit", [P, TT, E])
        prob = sb("prob", [P, TT, E])
        pick = sb("pick", [P, TT, E])
        pick2 = sb("pick2", [P, TT, E])
        rest = sb("rest", [P, TT, E])
        small = sb("small", [P, 6, TT])
        wts = [sb(f"wts{g}", [P, TT, E]) for g in range(G)]
        tanh_g = [sb(f"tanh_g{i}", [P, T]) for i in range(2)]
        gated = sb("gated", [P, T])
        hid = [sb(f"hid{i}", [P, T]) for i in range(2)]
        hid_hi = [sb(f"hid_hi{i}", [P, T], F32R) for i in range(2)]
        hid_lo = [sb(f"hid_lo{i}", [P, T], F32R) for i in range(2)]
        in_wk = sb("in_wk", [P, DC, H])

        ident = par[:, C_IDENT:C_IDENT + P]
        rank = par[:, C_RANK:C_RANK + E]
        dt_b = par[:, C_DTB:C_DTB + KH]
        d_skip = par[:, C_D:C_D + KH]
        in_w = par[:, C_INW:C_INW + H]
        xp_w = par[:, C_XPW:C_WG].rearrange("p (k c) -> p k c", k=KH)
        wg = par[:, C_WG:C_END].rearrange("p (k e) -> p k e", k=KH)
        taps = par[:, C_TAPS:C_IDENT].rearrange("p (j e) -> p j e", j=DC)

        ps_gate = [ps(f"ps_gate{i}", [P, T]) for i in range(2)]
        ps_up = [ps(f"ps_up{i}", [P, T]) for i in range(2)]
        ps_y = [ps(f"ps_y{i}", [P, TT // 2, H]) for i in range(2)]
        ps_b = ps("ps_b", [P, T])
        ps_c = ps("ps_c", [P, T])
        ps_sum = ps_up[1]
        ps_post = [ps_up, [ps_b, ps_c]]
        ps_logits = [ps_y[0][:, :, :].rearrange("p t h -> p (t h)"), ps_b]

        conv_w_in, ctx0_in, par_in = sem("conv_w_in"), sem("ctx0_in"), sem("par_in")
        x0_in, rest_in = sem("x0_in"), sem("rest_in")
        in_wk_done = sem("in_wk_done")
        w_in = [sem(f"w_in{m}") for m in range(MATS)]
        setup_pool, setup_exp, setup_dve = sem("setup_pool"), sem("setup_exp"), sem("setup_dve")
        conv_done = sem("conv_done")
        conv_taken = sem("conv_taken")
        u_done = sem("u_done")
        xdbl_done = sem("xdbl_done")
        dt_rows_done = sem("dt_rows_done")
        rows_hi_done = sem("rows_hi_done")
        rows_done = sem("rows_done")
        dtp_done = sem("dtp_done")
        abs_done = sem("abs_done")
        step_exp_done = sem("step_exp_done")
        step_w_done = sem("step_w_done")
        ln_done = sem("ln_done")
        step_rest_done = sem("step_rest_done")
        step_log_done = sem("step_log_done")
        delta_done = sem("delta_done")
        du_done = sem("du_done")
        z_done = sem("z_done")
        tanh_z_done = sem("tanh_z_done")
        gate2_done = sem("gate2_done")
        gated_z_done = sem("gated_z_done")
        acc_ready = sem("acc_ready")
        yg_done = sem("yg_done")
        yt_done = sem("yt_done")
        x2_done = sem("x2_done")
        x2t_done = sem("x2t_done")
        x2_s_done = sem("x2_s_done")
        x2_hi_done = sem("x2_hi_done")
        x2_lo_done = sem("x2_lo_done")
        logits_done = sem("logits_done")
        shifted = sem("shifted")
        exp_done = sem("exp_done")
        out_stored = sem("out_stored")
        pre_link = sem("pre_link")
        post_link = sem("post_link")
        b_done = sem("b_done")
        c_done = sem("c_done")
        decay_done = sem("decay_done")
        drive_done = [sem(f"drive_done{k}") for k in range(KH)]
        b_taken = sem("b_taken")
        scan_done = sem("scan_done")
        part_done = sem("part_done")
        sum_done = [sem(f"sum_done{k}") for k in range(KH)]
        gu_done = sem("gu_done")
        tanh_done = sem("tanh_done")
        gated_done = sem("gated_done")
        hid_done = sem("hid_done")
        hid_hi_done = sem("hid_hi_done")
        hid_lo_done = sem("hid_lo_done")
        down_done = sem("down_done")
        w_hi_done = sem("w_hi_done")
        split_done = sem("split_done")
        y_taken = sem("y_taken")
        final_lo_done = sem("final_lo_done")
        batch_down = sem("batch_down")
        batch_final = sem("batch_final")

        block = stack.enter_context(nc.Block())

        def split_job(r, last):
            at = r % IC
            if at == IC - 1 and last < 1:
                return 2, GATE
            if at < 2 and last < 2:
                return 1, UP + at
            return None

        @block.sync
        def _(sp):
            x_tiles = x.rearrange("b (t p) h -> p b t h", p=P)
            out_tiles = out.rearrange("b (t p) h -> p b t h", p=P)
            pad = DC - 1
            sp.dma_start(par[:, 0:C_IDENT], params[:, 0:C_IDENT]).then_inc(conv_w_in, 16)
            sp.dma_start(ctx_sb[:, 0:GB, pad:], ctx_t[:, 0:GB, :]).then_inc(ctx0_in, 16)
            sp.dma_start(par[:, C_IDENT:], params[:, C_IDENT:]).then_inc(par_in, 16)
            sp.dma_start(dtw[:, :], dt_w).then_inc(par_in, 16)
            sp.dma_start(x_sb[:, 0:GB].rearrange("p b t h -> p (b t) h"),
                         x_tiles[:, 0:GB].rearrange("p b t h -> p (b t) h")).then_inc(x0_in, 16)
            sp.dma_start(ctx_sb[:, GB:B, pad:], ctx_t[:, GB:B, :]).then_inc(rest_in, 16)
            sp.dma_start(x_sb[:, GB:B].rearrange("p b t h -> p (b t) h"),
                         x_tiles[:, GB:B].rearrange("p b t h -> p (b t) h")).then_inc(rest_in, 16)

            def load(n, e, m):
                sp.dma_start(w_raw[m][:, :], weights[e, m]).then_inc(w_in[m], 16)

            for m in range(MATS):
                load(0, 0, m)
            for first, end in ((1, X), (X, G * X)):
                with sp.Fori(first, end) as n:
                    for m in range(MATS):
                        sp.wait_ge(split_done, (n - 1) * MATS + m + 1)
                        load(n, n if first == 1 else n - X, m)
            for b in range(B):
                if b < B - GB:
                    sp.wait_ge(y_taken, (b // GB + 1) * X + 1)
                else:
                    sp.wait_ge(batch_final, b - (B - GB) + 1)
                sp.dma_start(out_tiles[:, b], x_sb[:, b]).then_inc(out_stored, 16)
            sp.wait_ge(out_stored, 16 * B)

        @block.tensor
        def _(pe):
            def convolve(g, halves=range(KH)):
                for k in halves:
                    if g == 0:
                        pe.wait_ge(in_wk_done, k + 1)
                    else:
                        pe.wait_ge(conv_taken, (g - 1) * KH + k + 1)
                    bank = ps_y[k][:, :, :].rearrange("p t h -> p (t h)")
                    for b in range(GB):
                        for j in range(DC):
                            mm = nc.tensor.matmul(bank[:, b * L:(b + 1) * L], in_wk[:, j, k * P:(k + 1) * P],
                                                  ctx_sb[:, g * GB + b, j:j + L], start=(b == 0 and j == 0),
                                                  stop=(j == DC - 1), skip_group_check=True)
                    mm.then_inc(conv_done, 1)

            def x_proj(g, halves=range(KH), batches=range(GB)):
                if g > 0 and (halves[0], batches[0]) == (0, 0):
                    pe.wait_ge(dt_rows_done, g)
                    pe.wait_ge(rows_done, g)
                for k in halves:
                    pe.wait_ge(u_done, g * KH + k + 1)
                    for b in batches:
                        at = slice(b * L, (b + 1) * L)
                        mm = nc.tensor.matmul(ps_up[0][0:XP, at], xp_w[:, k, :], u[g][:, k, at],
                                              start=(k == 0 and b == 0), stop=(k == KH - 1), skip_group_check=True)
                if (k, b) == (KH - 1, GB - 1):
                    mm.then_inc(xdbl_done, 1)

            def dt_proj(g, halves=range(KH), batches=range(GB)):
                pe.wait_ge(dt_rows_done, g + 1)
                for k in halves:
                    if g > 0:
                        pe.wait_ge(abs_done, (g - 1) * KH + k + 1)
                    for b in batches:
                        at = slice(b * L, (b + 1) * L)
                        mm = nc.tensor.matmul(ps_gate[k][:, at], dtw[:, k * P:(k + 1) * P], dt_rows[:, at],
                                              start=(b == 0), stop=True, skip_group_check=True)
                    if b == GB - 1:
                        mm.then_inc(dtp_done, 1)

            def spread(g, n, bank, first, done):
                nc.tensor.matmul(bank[:, :], sel[:, bass.ds(n + first, 1)].to_broadcast([PARTS * BC, P]),
                                 rows[g][:, :], start=True, stop=True).then_inc(done, 1)

            def spread_b(g, n):
                pe.wait_ge(drive_done[1], g * NS + n + 1)
                if g == 0:
                    pe.wait_ge(b_taken, n + 1)
                else:
                    pe.wait_ge(drive_done[0], g * NS + n + 1)
                spread(g, n, ps_b, 0, b_done)

            def spread_c(g, n):
                pe.wait_ge(part_done, g * UNITS + n * KH + 2)
                spread(g, n, ps_c, NS, c_done)

            def sum_init():
                pe.wait_ge(acc_ready, 1)
                nc.tensor.matmul(ps_sum[:, :], ident, u[0][:, 0, :], start=True, stop=True, skip_group_check=True)

            def sum_unit(n, odd):
                pe.wait_ge(part_done, n * KH + 3)
                nc.tensor.matmul(ps_sum[:, :], ident, part_odd[:, :] if odd else part[0][:, :], start=False,
                                 stop=True, skip_group_check=True).then_inc(sum_done[0], 1)

            def state_of_0(n):
                spread_c(0, n)
                spread_b(0, n + 1)
                sum_unit(n - 1, (n - 1) % 2)

            def spreads(g, first, end):
                with pe.Fori(first, end) as n:
                    spread_b(g, n)
                    spread_c(g, n)

            def transpose_y(g):
                pe.wait_ge(yg_done, g + 1)
                for b in range(GB):
                    bank = ps_post[g][b][:, :].rearrange("p (t h) -> p t h", t=TL)
                    for t in range(TL):
                        for k in range(KH):
                            at = b * L + t * P
                            mm = nc.tensor.transpose(bank[:, t, k * P:(k + 1) * P], yg[:, k, at:at + P], ident)
                    mm.then_inc(yt_done, 1)

            def transpose_x2(g):
                for t in range(TT):
                    pe.wait_ge(x2_done, g * TT + t + 1)
                    for k in range(KH):
                        at = k * L + t % TL * P
                        mm = nc.tensor.transpose(ps_post[g][t // TL][:, at:at + P], x2[:, t, k * P:(k + 1) * P], ident)
                    if t % TL == TL - 1:
                        mm.then_inc(x2t_done, 1)

            def logits(g, tiles=range(TT)):
                for t in tiles:
                    if t % TL == 0:
                        pe.wait_ge(x2_s_done, g * GB + t // TL + 1)
                    for k in range(KH):
                        mm = nc.tensor.matmul(ps_logits[g][:, t * E:(t + 1) * E], x2_s[:, k, t * P:(t + 1) * P],
                                              wg[:, k, :], start=(t == 0 and k == 0), stop=(k == KH - 1),
                                              skip_group_check=True)
                if t == TT - 1:
                    mm.then_inc(logits_done, 1)

            def gate_up(g, p, r):
                c, at, i = g * SLOTS + p * PAIR + r, r % IC, (r // IC + g) % 2
                if at == 0:
                    pe.wait_ge(split_done, expert(g, p, r) * MATS + UP + 1)
                pe.wait_ge(hid_done, c + 1)
                for bank, m in ((ps_gate[r % 2], GATE), (ps_up[r % 2], UP)):
                    todo = [(w, act, k) for w, act in ((w_hi, x2_hi), (w_lo, x2_hi), (w_hi, x2_lo)) for k in range(KH)]
                    for n, (w, act, k) in enumerate(todo):
                        col = k * I + at * P
                        if isinstance(p, int) and (p, r, m, n) == (0, 0, GATE, 2 * KH):
                            pe.wait_ge(x2_lo_done, g + 1)
                        mm = nc.tensor.matmul(bank[:, :], w[i][m][:, col:col + P], act[g][:, k, :],
                                              start=(n == 0), stop=(n == len(todo) - 1))
                mm.then_inc(gu_done, 1)

            def down(g, p, r):
                c, at, i = g * SLOTS + p * PAIR + r, r % IC, (r // IC + g) % 2
                if at == 0:
                    pe.wait_ge(split_done, expert(g, p, r) * MATS + DOWN + 1)
                    pe.wait_ge(y_taken, expert(g, p, r) + 1)
                final = g == G - 1 and isinstance(p, int) and (p, r) == (PAIRS, IC - 1)
                passes = list(enumerate(((hid_hi, w_hi), (hid_hi, w_lo), (hid_lo, w_hi))))
                if final:
                    pe.wait_ge(hid_hi_done, c + 1)
                    steps = [(t, passes[:2]) for t in range(TT)] + [(t, passes[2:]) for t in range(TT)]
                else:
                    pe.wait_ge(hid_lo_done, c + 3)
                    steps = [(t, passes) for t in range(TT)]
                for m, (t, todo) in enumerate(steps):
                    if final and m == TT:
                        pe.wait_ge(final_lo_done, 1)
                    for n, (h, w) in todo:
                        mm = nc.tensor.matmul(ps_y[t // 2][:, t % 2, :], h[r % 2][:, t * P:(t + 1) * P],
                                              w[i][DOWN][:, at * H:(at + 1) * H],
                                              start=(at == 0 and n == 0 and t % 2 == 0),
                                              stop=(at == IC - 1 and n == 2), skip_group_check=True)
                    if final and m >= TT and t % TL == TL - 1:
                        mm.then_inc(batch_down, 1)
                if not final:
                    mm.then_inc(down_done, 1)

            def expert(g, p, r):
                return g * X + p * 2 + r // IC

            def pair(g, p, states):
                for r in range(PAIR):
                    ahead = states and r % KH == 1
                    n = EARLY + p * (PAIR // KH) + (r + 1) // KH
                    if ahead:
                        spread_b(1, n)
                    gate_up(g, p, r + 2)
                    if ahead:
                        spread_c(1, n)
                    down(g, p, r)

            pe.wait_ge(setup_pool, 1)
            pe.wait_ge(ctx0_in, 16)
            convolve(0)
            pe.wait_ge(par_in, 32)
            x_proj(0)
            dt_proj(0)
            pe.wait_ge(rest_in, 32)
            convolve(1, [0])
            pe.wait_ge(rows_done, 1)
            pe.wait_ge(setup_pool, 4)
            spreads(0, 0, 1)
            convolve(1, [1])
            spread_b(0, 1)
            sum_init()
            for n in range(1, NS - 1):
                state_of_0(n)
                if STATE_XP <= n < STATE_XP + KH * GB:
                    x_proj(1, [(n - STATE_XP) // GB], [(n - STATE_XP) % GB])
                if STATE_DT <= n < STATE_DT + KH * GB:
                    dt_proj(1, [(n - STATE_DT) // GB], [(n - STATE_DT) % GB])
            spread_c(0, NS - 1)
            sum_unit(NS - 2, 0)
            pe.wait_ge(rows_done, G)
            pe.wait_ge(b_taken, NS + 1)
            spread_b(1, 0)
            sum_unit(NS - 1, 1)
            spread_c(1, 0)
            pe.wait_ge(abs_done, G * KH)
            assert EARLY == 3
            transpose_y(0)
            spread_b(1, 1)
            transpose_x2(0)
            spread_c(1, 1)
            logits(0, range(TL))
            spread_b(1, 2)
            logits(0, range(TL, TT))
            spread_c(1, 2)
            pe.wait_ge(x2_hi_done, 1)
            gate_up(0, 0, 0)
            spreads(1, EARLY, EARLY + 1)
            gate_up(0, 0, 1)
            for g in range(G):
                pair(g, 0, states=g == 0)
                with pe.Fori(1, PAIRS - 1) as p:
                    pair(g, p, states=g == 0)
                for r in range(PAIR):
                    gate_up(g, PAIRS - 1, r + 2)
                    down(g, PAIRS - 1, r)
                    if g == 0 and r == LATE:
                        transpose_y(1)
                    if g == 0 and r == LATE + 4:
                        transpose_x2(1)
                for r in range(IC):
                    if r < 2:
                        gate_up(g, PAIRS, r + 2)
                    elif g + 1 < G:
                        if r == 2:
                            pe.wait_ge(x2_hi_done, g + 2)
                        gate_up(g + 1, 0, r - 2)
                    down(g, PAIRS, r)
                    if g == 0 and r == 1:
                        logits(1)

        @block.scalar
        def _(act):
            def take_conv(g):
                for k in range(KH):
                    act.wait_ge(conv_done, g * KH + k + 1)
                    if g > 0:
                        act.wait_ge(delta_done, (g - 1) * KH + k + 1)
                    bank = ps_y[k][:, :, :].rearrange("p t h -> p (t h)")
                    nc.scalar.activation(conv_h[:, k, :], bank, ACT.Identity, bias=convb[:, k:k + 1], scale=0.5)
                    nc.scalar.activation(tanh_u[:, k, :], bank, ACT.Tanh, bias=convb[:, k:k + 1],
                                         scale=0.5).then_inc(conv_taken, 1)

            def take_z(g):
                act.wait_ge(z_done, g + 1)
                nc.scalar.activation(tanh_z[:, :, :], z[:, :, :], ACT.Tanh, scale=0.5).then_inc(tanh_z_done, 1)

            def take_rows(g):
                act.wait_ge(xdbl_done, g + 1)
                nc.scalar.copy(dt_rows[:, :], ps_up[0][PARTS * BC:XP, :]).then_inc(dt_rows_done, 1)
                nc.scalar.copy(rows[g][:, :], ps_up[0][0:PARTS * BC, :]).then_inc(rows_hi_done, 1)

            def take_step(g):
                for k in range(KH):
                    act.wait_ge(dtp_done, g * KH + k + 1)
                    act.wait_ge(u_done, g * KH + k + 1)
                    nc.scalar.activation(step_v[:, k, :], ps_gate[k][:, :], ACT.Identity, bias=dt_b[:, k:k + 1])
                    nc.scalar.activation(step_abs[:, k, :], ps_gate[k][:, :], ACT.Abs,
                                         bias=dt_b[:, k:k + 1]).then_inc(abs_done, 1)
                for k in range(KH):
                    act.wait_ge(abs_done, g * KH + k + 1)
                    nc.scalar.activation(step_e[:, k, :], step_abs[:, k, :], ACT.Exp, scale=-1.0).then_inc(step_exp_done, 1)
                for k in range(KH):
                    act.wait_ge(step_w_done, g * KH + k + 1)
                    nc.scalar.activation(step_ln[:, k, :], step_w[:, k, :], ACT.Ln).then_inc(ln_done, 1)

            def unit_decay(g, n, k):
                v = g * UNITS + n * KH + k
                act.wait_ge(scan_done, v + 1)
                dst = decay[k][:, :, 1:L]
                nc.scalar.activation(dst, delta[g][:, k, :].rearrange("p (b l) -> p b l", b=GB)[:, :, 1:L], ACT.Exp,
                                     scale=a_neg[:, k, bass.ds(n, 1)]).then_inc(decay_done, 1)

            def take_b(n):
                act.wait_ge(b_done, n + 1)
                act.wait_ge(drive_done[0], n + 1)
                nc.scalar.copy(b_row[:, :], ps_b[:, :]).then_inc(b_taken, 1)

            def state_decays(g, n):
                if g == 0:
                    take_b(n)
                act.wait_ge(delta_done, (g + 1) * KH)
                for k in range(KH):
                    unit_decay(g, n, k)

            def decays(g, first, end):
                with act.Fori(first, end) as n:
                    state_decays(g, n)

            def take_x2(g):
                for b in range(GB):
                    act.wait_ge(x2t_done, g * GB + b + 1)
                    nc.scalar.copy(x2_s[:, :, b * L:(b + 1) * L],
                                   ps_post[g][b][:, :].rearrange("p (k l) -> p k l", k=KH)).then_inc(x2_s_done, 1)
                act.wait_ge(x2_s_done, (g + 1) * GB)
                nc.scalar.copy(x2_hi[g][:, :, :], x2_s[:, :, :]).then_inc(x2_hi_done, 1)

            def router_exp(g):
                act.wait_ge(shifted, g + 1)
                nc.scalar.activation(prob[:, :, :], logit[:, :, :], ACT.Exp).then_inc(exp_done, 1)

            def split_hi(n, i, m):
                act.wait_ge(w_in[m], (n + 1) * 16)
                if not (isinstance(n, int) and n < 2):
                    if m == DOWN:
                        act.wait_ge(down_done, (n - 1) * IC + 2)
                    else:
                        act.wait_ge(gu_done, (n - 1) * IC)
                nc.scalar.copy(w_hi[i][m][:, :], w_raw[m][:, :]).then_inc(w_hi_done, 1)

            def gate_tanh(g, q, r):
                act.wait_ge(gu_done, g * SLOTS + q + 1)
                nc.scalar.activation(tanh_g[r % 2][:, :], ps_gate[r % 2][:, :], ACT.Tanh, scale=0.5).then_inc(tanh_done, 1)

            def round_hid(g, q, r):
                c = g * SLOTS + q
                act.wait_ge(hid_done, c + 3)
                act.wait_ge(down_done, c + 1)
                nc.scalar.copy(hid_hi[r % 2][:, :], hid[r % 2][:, :]).then_inc(hid_hi_done, 1)

            def slot(g, p, r, last=0, units=False):
                gate_tanh(g, p * PAIR + r, r)
                if units:
                    unit_decay(1, EARLY + p * (PAIR // KH) + r // KH, r % KH)
                if split_job(r, last):
                    ahead, m = split_job(r, last)
                    split_hi(g * X + p * 2 + r // IC + ahead, (r // IC + ahead + g) % 2, m)
                round_hid(g, p * PAIR + r, r)

            act.wait_ge(par_in, 32)
            nc.scalar.activation(a_neg[:, :, :], par[:, C_ALOG:C_D].rearrange("p (k n) -> p k n", k=KH),
                                 ACT.Exp).then_inc(setup_exp, 1)
            act.wait_ge(setup_dve, 1)
            act.sem_inc(b_taken, 1)
            take_conv(0)
            take_z(0)
            split_hi(0, 0, GATE)
            take_rows(0)
            split_hi(0, 0, UP)
            take_step(0)
            act.wait_ge(setup_dve, 2)
            act.wait_ge(setup_pool, 4)
            for n in range(CUTS[0]):
                state_decays(0, n)
            take_conv(1)
            split_hi(0, 0, DOWN)
            decays(0, CUTS[0], CUTS[1])
            take_rows(1)
            split_hi(1, 1, GATE)
            decays(0, CUTS[1], CUTS[2])
            take_step(1)
            take_z(1)
            decays(0, CUTS[2], NS)
            decays(1, 0, EARLY - 1)
            take_x2(0)
            decays(1, EARLY - 1, EARLY)
            router_exp(0)
            for g in range(G):
                for r in range(PAIR):
                    slot(g, 0, r, units=g == 0)
                with act.Fori(1, PAIRS - 1) as p:
                    for r in range(PAIR):
                        slot(g, p, r, units=g == 0)
                for r in range(PAIR):
                    slot(g, PAIRS - 1, r, last=g * (r // IC), units=g == 0 and r < LATE)
                for r in range(IC):
                    slot(g, PAIRS, r, last=2 * g)
                    if g == 0 and r == 0:
                        take_x2(1)
                    if g == 0 and r == 2:
                        router_exp(1)

        @block.gpsimd
        def _(pool):
            nc.gpsimd.memset(ctx_sb[:, :, 0:DC - 1], 0.0).then_inc(setup_pool, 1)
            for i in range(2):
                nc.gpsimd.memset(decay[i][:, :, 0:1], 0.0).then_inc(setup_pool, 1)
            pool.wait_ge(par_in, 32)
            nc.gpsimd.tensor_copy(sel[:, :], par[0:PARTS * BC, C_SEL:C_CONVB]).then_inc(setup_pool, 1)
            for k in range(KH):
                pool.sem_inc(sum_done[k], SUMS_AHEAD[k])
                pool.sem_inc(drive_done[k], 1)
            pool.sem_inc(hid_lo_done, 2)

            def start_sum(g):
                pool.wait_ge(xdbl_done, g + 1)
                pool.wait_ge(du_done, (g + 1) * KH)
                nc.gpsimd.tensor_tensor(u[g][:, :, :], u[g][:, :, :], d_skip.unsqueeze(2).to_broadcast([P, KH, T]),
                                        ALU.mult).then_inc(acc_ready, 1)
                pool.wait_ge(acc_ready, g + 1)

            def first_drive(n):
                pool.wait_ge(b_taken, n + 2)
                pool.wait_ge(scan_done, n * KH + 1)
                nc.gpsimd.tensor_tensor(drive[0][:, :], du[0][:, 0, :], b_row[:, :], ALU.mult).then_inc(drive_done[0], 1)

            def add_unit(g, n, k):
                pool.wait_ge(part_done, g * UNITS + n * KH + k + 3)
                pool.wait_ge(sum_done[k], g * NS + n + SUMS_AHEAD[k])
                nc.gpsimd.tensor_tensor(u[g][:, k, :], u[g][:, k, :], part[k][:, :], ALU.add).then_inc(sum_done[k], 1)

            def states_of_0(first, end):
                with pool.Fori(first, end) as n:
                    first_drive(n + 1)
                    add_unit(0, n, 1)

            def sums(g, first, end):
                with pool.Fori(first, end) as n:
                    for k in range(KH):
                        add_unit(g, n, k)

            def split_lo(n, i, m):
                pool.wait_ge(w_hi_done, n * MATS + m + 1)
                nc.gpsimd.tensor_tensor(w_lo[i][m][:, :], w_raw[m][:, :], w_hi[i][m][:, :].bitcast(F32),
                                        ALU.subtract).then_inc(split_done, 1)

            def rest_hid(g, q, r):
                pool.wait_ge(hid_hi_done, g * SLOTS + q + 1)
                nc.gpsimd.tensor_tensor(hid_lo[r % 2][:, :], hid[r % 2][:, :], hid_hi[r % 2][:, :].bitcast(F32),
                                        ALU.subtract).then_inc(hid_lo_done, 1)

            def pre_gate_1():
                pool.wait_ge(tanh_z_done, 2)
                nc.gpsimd.tensor_tensor(tanh_z[:, :, :], tanh_z[:, :, :], z[:, :, :], ALU.mult).then_inc(gated_z_done, 1)
                pool.wait_ge(gated_z_done, 1)
                nc.gpsimd.tensor_tensor(gate2[1][:, :, :], tanh_z[:, :, :], z[:, :, :], ALU.add).then_inc(gate2_done, 1)

            def rest_x2(g):
                pool.wait_ge(x2_hi_done, g + 1)
                nc.gpsimd.tensor_tensor(x2_lo[g][:, :, :], x2_s[:, :, :], x2_hi[g][:, :, :].bitcast(F32),
                                        ALU.subtract).then_inc(x2_lo_done, 1)

            def slot(g, p, r, last=0, units=False):
                if not (isinstance(p, int) and (g, p, r) == (G - 1, PAIRS, IC - 1)):
                    rest_hid(g, p * PAIR + r, r)
                if split_job(r, last):
                    ahead, m = split_job(r, last)
                    split_lo(g * X + p * 2 + r // IC + ahead, (r // IC + ahead + g) % 2, m)
                if units:
                    add_unit(1, EARLY + p * (PAIR // KH) + r // KH, r % KH)

            split_lo(0, 0, GATE)
            split_lo(0, 0, UP)
            pool.wait_ge(du_done, 1)
            first_drive(0)
            start_sum(0)
            states_of_0(0, CUTS[2] - 1)
            split_lo(0, 0, DOWN)
            split_lo(1, 1, GATE)
            states_of_0(CUTS[2] - 1, NS - 1)
            add_unit(0, NS - 1, 1)
            start_sum(1)
            pre_gate_1()
            sums(1, 0, 1)
            rest_x2(0)
            sums(1, 1, EARLY)
            for g in range(G):
                for r in range(PAIR):
                    slot(g, 0, r, units=g == 0)
                with pool.Fori(1, PAIRS - 1) as p:
                    for r in range(PAIR):
                        slot(g, p, r, units=g == 0)
                for r in range(PAIR):
                    slot(g, PAIRS - 1, r, last=g * (r // IC), units=g == 0 and r < LATE)
                for r in range(IC):
                    slot(g, PAIRS, r, last=2 * g)
                    if g == 0 and r == 0:
                        rest_x2(1)

        @block.vector
        def _(dve):
            links = {}

            def link(ins, chain):
                links[chain.name] = links.get(chain.name, 0) + 1
                ins.then_inc(chain, 1)
                dve.wait_ge(chain, links[chain.name])

            def pre(ins):
                link(ins, pre_link)

            def post(ins):
                link(ins, post_link)

            def rsqrt(tiles, step):
                at = slice(tiles[0], tiles[-1] + 1)
                v, i, r = ve[:, at], yi[:, at], nr[:, at]
                y = i.bitcast(F32)
                step(nc.vector.tensor_scalar(v, mv[:, at, 1], EPS, None, ALU.add))
                step(nc.vector.tensor_scalar(i, v.bitcast(I32), 1, None, ALU.logical_shift_right))
                step(nc.vector.tensor_scalar(i, i, -1.0, float(SEED), ALU.mult, ALU.add))
                for _ in range(3):
                    step(nc.vector.scalar_tensor_tensor(out=r, in0=y, scalar=-0.5, in1=y, op0=ALU.mult, op1=ALU.mult))
                    step(nc.vector.tensor_tensor(r, r, v, ALU.mult))
                    step(nc.vector.scalar_tensor_tensor(out=y, in0=r, scalar=1.5, in1=y, op0=ALU.add, op1=ALU.mult))

            def moments(tiles, step):
                for t in tiles:
                    if step is pre and t == TT:
                        dve.wait_ge(rest_in, 32)
                    ins = nc.vector.bn_stats(stats[:, t, :], x_sb[:, t // TL, t % TL, :])
                step(ins)
                for t in tiles:
                    ins = nc.vector.bn_aggr(mv[:, t, :], stats[:, t, :])
                step(ins)

            def normed(g, dst, tile_done=None):
                for t in range(TT):
                    n = g * TT + t
                    ins = nc.vector.tensor_scalar(dst(t), x_sb[:, n // TL, n % TL, :], mv[:, n, 0:1],
                                                  yi[:, n:n + 1].bitcast(F32), ALU.subtract, ALU.mult)
                    if tile_done is not None:
                        ins.then_inc(tile_done, 1)
                return ins

            def pre_norm(g):
                if g > 0:
                    dve.wait_ge(gate2_done, g)
                normed(g, lambda t: z[:, t % TL, (t // TL) * L:(t // TL + 1) * L]).then_inc(z_done, 1)

            def pre_u(g, halves=range(KH)):
                for k in halves:
                    dve.wait_ge(conv_taken, g * KH + k + 1)
                    nc.vector.scalar_tensor_tensor(out=u[g][:, k, :], in0=tanh_u[:, k, :], scalar=1.0,
                                                   in1=conv_h[:, k, :], op0=ALU.add, op1=ALU.mult).then_inc(u_done, 1)

            def pre_gate(g):
                dve.wait_ge(tanh_z_done, g + 1)
                nc.vector.scalar_tensor_tensor(out=gate2[g][:, :, :], in0=tanh_z[:, :, :], scalar=1.0,
                                               in1=z[:, :, :], op0=ALU.add, op1=ALU.mult).then_inc(gate2_done, 1)

            def pre_rows(g):
                a, b, c = (slice(n * BC, (n + 1) * BC) for n in range(PARTS))
                dve.wait_ge(rows_hi_done, g + 1)
                nc.vector.tensor_tensor(row_rest[c, :], ps_up[0][c, :], rows[g][c, :], ALU.subtract)
                pre(nc.vector.tensor_tensor(rows[g][b, :], ps_up[0][b, :], rows[g][b, :], ALU.subtract))
                pre(nc.vector.tensor_copy(row_mid[c, :], row_rest[c, :]))
                nc.vector.tensor_tensor(rows[g][c, :], row_rest[c, :], row_mid[c, :],
                                        ALU.subtract).then_inc(rows_done, 1)

            def halves(g):
                return [(k, g * KH + k + 1) for k in range(KH)]

            def pre_rest(g):
                for k, count in halves(g):
                    dve.wait_ge(step_exp_done, count)
                    nc.vector.tensor_scalar(step_w[:, k, :], step_e[:, k, :], 1.0, None, ALU.add).then_inc(step_w_done, 1)
                for k, count in halves(g):
                    dve.wait_ge(step_w_done, count)
                    nc.vector.scalar_tensor_tensor(out=step_e[:, k, :], in0=step_w[:, k, :], scalar=-1.0,
                                                   in1=step_e[:, k, :], op0=ALU.add,
                                                   op1=ALU.subtract).then_inc(step_rest_done, 1)

            def pre_step(g):
                for k, count in halves(g):
                    dve.wait_ge(step_rest_done, count)
                    dve.wait_ge(ln_done, count)
                    nc.vector.tensor_tensor(step_e[:, k, :], step_ln[:, k, :], step_e[:, k, :],
                                            ALU.subtract).then_inc(step_log_done, 1)
                for k, count in halves(g):
                    dve.wait_ge(step_log_done, count)
                    nc.vector.scalar_tensor_tensor(out=delta[g][:, k, :], in0=step_v[:, k, :], scalar=0.0,
                                                   in1=step_e[:, k, :], op0=ALU.max, op1=ALU.add).then_inc(delta_done, 1)
                for k, count in halves(g):
                    dve.wait_ge(delta_done, count)
                    nc.vector.tensor_tensor(du[g][:, k, :], delta[g][:, k, :], u[g][:, k, :],
                                            ALU.mult).then_inc(du_done, 1)

            def unit_drive(g, n, k):
                if g == 0:
                    dve.wait_ge(b_taken, n + 2)
                else:
                    dve.wait_ge(b_done, NS + n + 1)
                dve.wait_ge(scan_done, g * UNITS + n * KH + k + 1)
                nc.vector.tensor_tensor(drive[k][:, :], du[g][:, k, :], ps_b[:, :], ALU.mult).then_inc(drive_done[k], 1)

            def unit_scan(g, n, k):
                v = g * UNITS + n * KH + k
                dve.wait_ge(drive_done[k], g * NS + n + 2)
                dve.wait_ge(decay_done, v + 1)
                dve.wait_ge(part_done, v + 1)
                nc.vector.tensor_tensor_scan(state[k][:, :], decay[k][:, :, :].rearrange("p b l -> p (b l)"),
                                             drive[k][:, :], 0.0, ALU.mult, ALU.add).then_inc(scan_done, 1)

            def unit_part(g, n, k, odd=0):
                dve.wait_ge(c_done, g * NS + n + 1)
                dve.wait_ge(scan_done, g * UNITS + n * KH + k + 3)
                dve.wait_ge(sum_done[k], g * NS + n + (1 if g == 0 else SUMS_AHEAD[k]))
                dst = part_odd if odd and k == 0 else part[k]
                nc.vector.tensor_tensor(dst[:, :], state[k][:, :], ps_c[:, :], ALU.mult).then_inc(part_done, 1)

            def units_of_0(first, end):
                dve.wait_ge(du_done, KH)
                with dve.Fori(0, (end - first) // 2) as m:
                    for odd in range(2):
                        n = m * 2 + (first + odd)
                        unit_drive(0, n, 1)
                        for k in range(KH):
                            unit_scan(0, n, k)
                        for k in range(KH):
                            unit_part(0, n, k, odd)

            def units_of_1(first, end):
                dve.wait_ge(du_done, G * KH)
                with dve.Fori(first, end) as n:
                    for step in (unit_drive, unit_scan, unit_part):
                        for k in range(KH):
                            step(1, n, k)

            def post_gate(g):
                dve.wait_ge(gate2_done, g + 1)
                for k in range(KH):
                    dve.wait_ge(sum_done[k], (g + 1) * NS + SUMS_AHEAD[k])
                    y = ps_sum[:, :] if (g, k) == (0, 0) else u[g][:, k, :]
                    ins = nc.vector.scalar_tensor_tensor(out=yg[:, k, :], in0=y, scalar=0.5, in1=gate2[g][:, k, :],
                                                         op0=ALU.mult, op1=ALU.mult)
                ins.then_inc(yg_done, 1)

            def post_add(g):
                for b in range(GB):
                    dve.wait_ge(yt_done, g * GB + b + 1)
                    xb = x_sb[:, g * GB + b].rearrange("p t h -> p (t h)")
                    ins = nc.vector.tensor_tensor(xb, xb, ps_post[g][b][:, :], ALU.add)
                post(ins)

            def post_norm(g):
                normed(g, lambda t: x2[:, t, :], x2_done)

            def wide(ap):
                return ap.unsqueeze(2).to_broadcast([P, TT, E])

            ranks = rank.unsqueeze(1).to_broadcast([P, TT, E])
            top, total, first, second, mark, share = (small[:, n, :] for n in range(6))

            def route_exp(g):
                dve.wait_ge(logits_done, g + 1)
                lg = ps_logits[g][:, 0:TT * E].rearrange("p (t e) -> p t e", t=TT)
                post(nc.vector.tensor_reduce(top, lg, AX_X, ALU.max))
                nc.vector.tensor_tensor(logit[:, :, :], lg, wide(top), ALU.subtract).then_inc(shifted, 1)

            def route_first(g):
                dve.wait_ge(exp_done, g + 1)
                post(nc.vector.tensor_reduce(total, prob[:, :, :], AX_X, ALU.add))
                post(nc.vector.reciprocal(total, total))
                post(nc.vector.tensor_tensor(prob[:, :, :], prob[:, :, :], wide(total), ALU.mult))
                post(nc.vector.tensor_reduce(first, prob[:, :, :], AX_X, ALU.max))
                post(nc.vector.tensor_tensor(pick[:, :, :], prob[:, :, :], wide(first), ALU.is_equal))
                post(nc.vector.tensor_tensor(pick[:, :, :], pick[:, :, :], ranks, ALU.mult))
                post(nc.vector.tensor_reduce(mark, pick[:, :, :], AX_X, ALU.max))
                post(nc.vector.tensor_tensor(pick[:, :, :], ranks, wide(mark), ALU.is_equal))

            def route_second(g):
                post(nc.vector.scalar_tensor_tensor(out=rest[:, :, :], in0=pick[:, :, :], scalar=-2.0,
                                                    in1=prob[:, :, :], op0=ALU.mult, op1=ALU.add))
                post(nc.vector.tensor_reduce(second, rest[:, :, :], AX_X, ALU.max))
                post(nc.vector.tensor_tensor(pick2[:, :, :], rest[:, :, :], wide(second), ALU.is_equal))
                post(nc.vector.tensor_tensor(pick2[:, :, :], pick2[:, :, :], ranks, ALU.mult))
                post(nc.vector.tensor_reduce(mark, pick2[:, :, :], AX_X, ALU.max))
                post(nc.vector.tensor_tensor(pick2[:, :, :], ranks, wide(mark), ALU.is_equal))

            def route_weights(g):
                post(nc.vector.tensor_tensor(share, first, second, ALU.add))
                post(nc.vector.tensor_scalar(share, share, 2.0, None, ALU.mult))
                post(nc.vector.reciprocal(share, share))
                post(nc.vector.tensor_tensor(pick[:, :, :], pick[:, :, :], pick2[:, :, :], ALU.add))
                post(nc.vector.tensor_tensor(pick[:, :, :], pick[:, :, :], prob[:, :, :], ALU.mult))
                post(nc.vector.tensor_tensor(wts[g][:, :, :], pick[:, :, :], wide(share), ALU.mult))

            def gate_mul(g, q, r):
                dve.wait_ge(tanh_done, g * SLOTS + q + 1)
                dve.wait_ge(hid_done, g * SLOTS + q + 2)
                nc.vector.scalar_tensor_tensor(out=gated[:, :], in0=tanh_g[r % 2][:, :], scalar=1.0,
                                               in1=ps_gate[r % 2][:, :], op0=ALU.add, op1=ALU.mult).then_inc(gated_done, 1)

            def up_mul(g, q, r):
                dve.wait_ge(gated_done, g * SLOTS + q + 1)
                dve.wait_ge(hid_lo_done, g * SLOTS + q + 1)
                nc.vector.tensor_tensor(hid[r % 2][:, :], gated[:, :], ps_up[r % 2][:, :], ALU.mult).then_inc(hid_done, 1)

            def add_expert(g, e):
                dve.wait_ge(down_done, g * SLOTS + e * IC + IC + 2)
                add_tiles(g, e, range(TT)).then_inc(y_taken, 1)

            def add_tiles(g, e, tiles):
                for t in tiles:
                    weight = 0.5 if isinstance(e, int) and e == E else wts[g][:, t, bass.ds(e, 1)]
                    xt = x_sb[:, g * GB + t // TL, t % TL, :]
                    ins = nc.vector.scalar_tensor_tensor(out=xt, in0=ps_y[t // 2][:, t % 2, :], scalar=weight,
                                                         in1=xt, op0=ALU.mult, op1=ALU.add)
                return ins

            def slot(g, p, r, units=False):
                unit = (1, EARLY + p * (PAIR // KH) + r // KH, r % KH)
                gate_mul(g, p * PAIR + r, r)
                if r % IC == 1:
                    if isinstance(p, int) and p == 0 and r == 1:
                        if g > 0:
                            add_expert(g - 1, E)
                    else:
                        add_expert(g, p * 2 + r // IC - 1)
                if units:
                    unit_drive(*unit)
                up_mul(g, p * PAIR + r, r)
                if units:
                    unit_scan(*unit)
                    unit_part(*unit)

            dve.wait_ge(conv_w_in, 16)
            for k in range(KH):
                half = slice(k * P, (k + 1) * P)
                nc.vector.tensor_tensor(in_wk[:, :, half], taps[:, :, half],
                                        in_w[:, half].unsqueeze(1).to_broadcast([P, DC, P]),
                                        ALU.mult).then_inc(in_wk_done, 1)
            dve.wait_ge(par_in, 32)
            nc.vector.tensor_scalar(convb[:, :], par[:, C_CONVB:C_DTB], 0.5, None, ALU.mult).then_inc(setup_dve, 1)
            dve.wait_ge(setup_exp, 1)
            nc.vector.tensor_scalar(a_neg[:, :, :], a_neg[:, :, :], -1.0, None, ALU.mult).then_inc(setup_dve, 1)
            for s, n in ((hid_done, 2), (down_done, 2), (scan_done, 2), (part_done, 2), (y_taken, 1)):
                dve.sem_inc(s, n)
            dve.wait_ge(x0_in, 16)
            moments(range(B * TL), pre)
            rsqrt(range(B * TL), pre)
            pre_u(0, [0])
            pre_norm(0)
            pre_u(0, [1])
            pre_rows(0)
            pre_gate(0)
            pre_rest(0)
            pre_step(0)
            units_of_0(0, CUTS[0])
            pre_u(1)
            pre_norm(1)
            units_of_0(CUTS[0], CUTS[1])
            pre_rows(1)
            units_of_0(CUTS[1], CUTS[2])
            pre_rest(1)
            pre_step(1)
            units_of_0(CUTS[2], NS)
            dve.wait_ge(du_done, G * KH)
            for k in range(KH):
                unit_drive(1, 0, k)
            post_gate(0)
            for k in range(KH):
                unit_scan(1, 0, k)
            post_add(0)
            moments(range(TT), post)
            rsqrt(range(TT), post)
            post_norm(0)
            for k in range(KH):
                unit_part(1, 0, k)
            units_of_1(1, EARLY)
            route_exp(0)
            for g in range(G):
                for r in range(PAIR):
                    slot(g, 0, r, units=g == 0)
                    if g == 0 and r == 0:
                        route_first(0)
                    if r == 1:
                        route_second(g)
                    if r == 2:
                        route_weights(g)
                with dve.Fori(1, PAIRS - 1) as p:
                    for r in range(PAIR):
                        slot(g, p, r, units=g == 0)
                for r in range(PAIR):
                    slot(g, PAIRS - 1, r, units=g == 0 and r < LATE)
                    if g == 0 and r == LATE:
                        post_gate(1)
                    if g == 0 and r == LATE + 1:
                        post_add(1)
                    if g == 0 and r == LATE + 2:
                        moments(range(TT, G * TT), post)
                    if g == 0 and r == LATE + 3:
                        rsqrt(range(TT, G * TT), post)
                    if g == 0 and r == LATE + 4:
                        post_norm(1)
                for r in range(IC):
                    slot(g, PAIRS, r)
                    if g == 0 and r == 2:
                        route_exp(1)
                    if g == 0 and r == 3:
                        route_first(1)
            dve.wait_ge(hid_hi_done, G * SLOTS)
            r = (SLOTS - 1) % 2
            nc.vector.tensor_tensor(hid_lo[r][:, :], hid[r][:, :], hid_hi[r][:, :].bitcast(F32),
                                    ALU.subtract).then_inc(final_lo_done, 1)
            for b in range(GB):
                dve.wait_ge(batch_down, b + 1)
                add_tiles(G - 1, E, range(b * TL, (b + 1) * TL)).then_inc(batch_final, 1)


def kernel(x, ctx_1024, L0_xattn_in_proj_w, L0_xattn_conv_w, L0_xattn_conv_b, L0_xattn_x_proj_w,
           L0_xattn_dt_proj_w, L0_xattn_dt_proj_b, L0_xattn_A_log, L0_xattn_D, L0_ffn_wg, L0_ffn_gate_w,
           L0_ffn_up_w, L0_ffn_down_w, L0_ffn_shared_gate_w, L0_ffn_shared_up_w, L0_ffn_shared_down_w):
    import numpy as np
    import concourse.bacc as bacc
    from concourse.bass_utils import run_bass_kernel_spmd

    def halves(a):
        a = np.asarray(a).reshape(-1, P, int(np.prod(np.shape(a)[1:], dtype=int)))
        return a.transpose(1, 0, 2).reshape(P, -1)

    xp = np.asarray(L0_xattn_x_proj_w).T
    xp = np.concatenate([xp[:, DR:]] * PARTS + [xp[:, :DR]], axis=1)
    sel = np.zeros((P, BC), np.float32)
    sel[:PARTS * BC] = np.tile(np.eye(BC, dtype=np.float32), (PARTS, 1))
    params = np.concatenate([
        np.asarray(L0_xattn_in_proj_w).T, np.tile(np.asarray(L0_xattn_conv_w).T.reshape(1, -1), (P, 1)),
        np.eye(P, dtype=np.float32),
        np.tile(np.arange(E, 0, -1, dtype=np.float32), (P, 1)), sel,
        halves(L0_xattn_conv_b), halves(L0_xattn_dt_proj_b), halves(L0_xattn_A_log),
        halves(L0_xattn_D), halves(xp), halves(np.asarray(L0_ffn_wg).T)], axis=1)
    gate = np.concatenate([np.asarray(L0_ffn_gate_w), np.asarray(L0_ffn_shared_gate_w)[None]])
    up = np.concatenate([np.asarray(L0_ffn_up_w), np.asarray(L0_ffn_shared_up_w)[None]])
    down = np.concatenate([np.asarray(L0_ffn_down_w), np.asarray(L0_ffn_shared_down_w)[None]])
    weights = np.stack([np.stack([halves(gate[e]), halves(up[e]), halves(down[e])]) for e in range(X)])
    arrays = {
        "x": np.ascontiguousarray(x),
        "ctx_t": np.ascontiguousarray(np.asarray(ctx_1024).transpose(2, 0, 1)),
        "params": np.ascontiguousarray(params),
        "dt_w": np.ascontiguousarray(np.asarray(L0_xattn_dt_proj_w).T),
        "weights": np.ascontiguousarray(weights),
    }
    nc = bacc.Bacc("TRN2", target_bir_lowering=False, num_devices=1)
    args = [nc.dram_tensor(name, a.shape, mybir.dt.from_np(a.dtype), kind="ExternalInput").ap()
            for name, a in arrays.items()]
    args.append(nc.dram_tensor("out", (B, L, H), F32, kind="ExternalOutput").ap())
    build(nc, *args)
    result = run_bass_kernel_spmd(nc, [arrays], core_ids=[0])
    return result.results[0]["out"]
```
